# Optimizing a Trainium2 kernel written in Bass

```python
import numpy as np
import jax
import jax.numpy as jnp

def _softmax(x, axis=-1):
    return jax.nn.softmax(x, axis=axis)

def _gelu(x):
    return jax.nn.gelu(x, approximate=True)

def _silu(x):
    return jax.nn.silu(x)

def _sigmoid(x):
    return jax.nn.sigmoid(x)

def _layernorm(x, axis=-1, eps=1e-05):
    m = jnp.mean(x, axis=axis, keepdims=True)
    v = jnp.var(x, axis=axis, keepdims=True)
    return (x - m) / jnp.sqrt(v + eps)

def _scatter_add(tgt, idx, src, axis=0):
    return tgt.at[idx].add(src)

def _segment_sum(src, seg, n):
    return jax.ops.segment_sum(src, seg, n)
kernel_name = 'mk_xattn_ffn_d1_seqx_r4_41db5a'

def setup_inputs(seed: int=0):
    np.random.seed(seed)
    _w = jnp.asarray

    def _rec_inputs():
        import jax
        import jax.numpy as jnp
        _rk = jax.random.key(seed)
        x = -0.0002928 + 1 * jax.random.normal(jax.random.fold_in(_rk, 1), (8, 256, 256), jnp.float32)
        _lenS = 256 - jax.random.randint(jax.random.fold_in(_rk, 7), (8,), 0, max(1, 256 // 4) + 1, jnp.int32)
        _lenS2 = 120 - jax.random.randint(jax.random.fold_in(_rk, 8), (8,), 0, max(1, 120 // 4) + 1, jnp.int32)
        _ctx_1024P = jax.random.normal(jax.random.fold_in(_rk, 11), (8, 16, 256), jnp.float32)
        _ctx_1024c = jax.random.dirichlet(jax.random.fold_in(_rk, 511), 0.3 * jnp.ones((16,), jnp.float32), (8, 120))
        _ctx_1024t = jnp.einsum('bsk,bkd->bsd', _ctx_1024c, _ctx_1024P)
        _ctx_1024t = _ctx_1024t * jax.lax.rsqrt(jnp.mean(jnp.square(_ctx_1024t)) + 1e-12) * 0.953939
        ctx_1024 = -1.39393e-06 + 0.999914 * (_ctx_1024t + 0.3 * jax.random.normal(jax.random.fold_in(_rk, 611), (8, 120, 256), jnp.float32))
        _validS = jnp.arange(256)[None, :] < _lenS[:, None]
        _validS2 = jnp.arange(120)[None, :] < _lenS2[:, None]
        _causal = jnp.tril(jnp.ones((256, 256), dtype=bool))
        mask_SxS2_bk1 = jnp.broadcast_to(_validS2[0:1, :], (256, 120))
        mask_BxS2_bf0 = jnp.logical_not(jnp.ones((8, 120), dtype=bool))
        return (x, ctx_1024, mask_SxS2_bk1, mask_BxS2_bf0)
    x, ctx_1024, mask_SxS2_bk1, mask_BxS2_bf0 = _rec_inputs()

    def _L0_xattn_setup():
        import jax, jax.numpy as jnp
        import numpy as np
        B, T, D, H = (2, 512, 256, 16)
        DK = D // H
        SCALE = 1.0 / float(np.sqrt(DK))
        key0 = jax.random.key(seed)
        ks = jax.random.split(key0, 12)
        std = 0.02
        inp = {'query': jax.random.normal(ks[0], (B, T, D), jnp.float32), 'key': jax.random.normal(ks[1], (B, T, D), jnp.float32), 'value': jax.random.normal(ks[2], (B, T, D), jnp.float32), 'Wq': jax.random.normal(ks[3], (D, D), jnp.float32) * std, 'bq': jnp.zeros((D,), jnp.float32), 'Wk': jax.random.normal(ks[4], (D, D), jnp.float32) * std, 'bk': jnp.zeros((D,), jnp.float32), 'Wv': jax.random.normal(ks[5], (D, D), jnp.float32) * std, 'bv': jnp.zeros((D,), jnp.float32), 'Wo': jax.random.normal(ks[6], (D, D), jnp.float32) * std, 'bo': jnp.zeros((D,), jnp.float32), 'attn_mask': jnp.triu(jnp.ones((T, T), jnp.bool_), k=1), 'key_padding_mask': jnp.zeros((B, T), jnp.bool_)}
        return inp
    _L0_xattn_all = _L0_xattn_setup()
    _L0_xattn_in = {k: v for k, v in _L0_xattn_all.items() if k in ('Wq', 'bq', 'Wk', 'bk', 'Wv', 'bv', 'Wo', 'bo')}
    del _L0_xattn_all

    def _L0_ffn_setup():
        import jax, jax.numpy as jnp
        import numpy as np
        B, S, H, E = (4, 512, 256, 8)
        key = jax.random.key(seed)
        k1, k2, k3 = jax.random.split(key, 3)
        scale = 1.0 / np.sqrt(H)
        return {'x': jax.random.normal(k1, (B, S, H), dtype=jnp.float32), 'router_w': jax.random.normal(k2, (H, E), dtype=jnp.float32) * scale, 'router_b': jnp.zeros((E,), dtype=jnp.float32), 'expert_w': jax.random.normal(k3, (E, H, H), dtype=jnp.float32) * scale, 'expert_b': jnp.zeros((E, H), dtype=jnp.float32)}
    _L0_ffn_all = _L0_ffn_setup()
    _L0_ffn_in = {k: v for k, v in _L0_ffn_all.items() if k in ('router_w', 'router_b', 'expert_w', 'expert_b')}
    del _L0_ffn_all
    return {'x': x, 'ctx_1024': ctx_1024, 'mask_SxS2_bk1': mask_SxS2_bk1, 'mask_BxS2_bf0': mask_BxS2_bf0, 'L0_xattn_Wq': _L0_xattn_in['Wq'], 'L0_xattn_bq': _L0_xattn_in['bq'], 'L0_xattn_Wk': _L0_xattn_in['Wk'], 'L0_xattn_bk': _L0_xattn_in['bk'], 'L0_xattn_Wv': _L0_xattn_in['Wv'], 'L0_xattn_bv': _L0_xattn_in['bv'], 'L0_xattn_Wo': _L0_xattn_in['Wo'], 'L0_xattn_bo': _L0_xattn_in['bo'], 'L0_ffn_router_w': _L0_ffn_in['router_w'], 'L0_ffn_router_b': _L0_ffn_in['router_b'], 'L0_ffn_expert_w': _L0_ffn_in['expert_w'], 'L0_ffn_expert_b': _L0_ffn_in['expert_b']}

def reference(x, ctx_1024, mask_SxS2_bk1, mask_BxS2_bf0, L0_xattn_Wq, L0_xattn_bq, L0_xattn_Wk, L0_xattn_bk, L0_xattn_Wv, L0_xattn_bv, L0_xattn_Wo, L0_xattn_bo, L0_ffn_router_w, L0_ffn_router_b, L0_ffn_expert_w, L0_ffn_expert_b):
    import jax
    import jax.numpy as jnp

    def _L0_xattn_ref(query, key, value, Wq, bq, Wk, bk, Wv, bv, Wo, bo, attn_mask, key_padding_mask):
        import jax, jax.numpy as jnp
        import numpy as np
        B, T, D, H = (2, 512, 256, 16)
        DK = D // H
        SCALE = 1.0 / float(np.sqrt(DK))
        Bq, Tq, _ = query.shape
        Tk = key.shape[1]
        q = (query @ Wq.T + bq).reshape(Bq, Tq, H, DK)
        k = (key @ Wk.T + bk).reshape(Bq, Tk, H, DK)
        v = (value @ Wv.T + bv).reshape(Bq, Tk, H, DK)
        scores = jnp.einsum('bqhd,bkhd->bhqk', q, k) * jnp.float32(SCALE)
        neg_inf = jnp.float32(-jnp.inf)
        scores = jnp.where(attn_mask[None, None, :, :], neg_inf, scores)
        scores = jnp.where(key_padding_mask[:, None, None, :], neg_inf, scores)
        attn = jax.nn.softmax(scores, axis=-1)
        out = jnp.einsum('bhqk,bkhd->bqhd', attn, v).reshape(Bq, Tq, D)
        return out @ Wo.T + bo

    def _L0_ffn_ref(x, router_w, router_b, expert_w, expert_b):
        import jax, jax.numpy as jnp
        import numpy as np
        B, S, H, E = (4, 512, 256, 8)
        b, s, h = x.shape
        hs = x.reshape(-1, h)
        logits = hs @ router_w + router_b
        probs = jax.nn.softmax(logits, axis=-1)
        idx = jnp.argmax(probs, axis=-1)
        gate = jnp.take_along_axis(probs, idx[:, None], axis=-1)
        expert_out = jnp.einsum('th,ehd->ted', hs, expert_w) + expert_b
        dispatch = jax.nn.one_hot(idx, expert_w.shape[0], dtype=hs.dtype) * gate
        out = jnp.einsum('te,ted->td', dispatch, expert_out)
        return out.reshape(b, s, h)
    x = x + _L0_xattn_ref(_layernorm(x, axis=-1), ctx_1024, ctx_1024, L0_xattn_Wq, L0_xattn_bq, L0_xattn_Wk, L0_xattn_bk, L0_xattn_Wv, L0_xattn_bv, L0_xattn_Wo, L0_xattn_bo, mask_SxS2_bk1, mask_BxS2_bf0)
    x = x + _L0_ffn_ref(_layernorm(x, axis=-1), L0_ffn_router_w, L0_ffn_router_b, L0_ffn_expert_w, L0_ffn_expert_b)
    return x

_drawn_inputs = setup_inputs


def setup_inputs(seed=0):
    import zlib

    import numpy as np

    out = dict(_drawn_inputs(seed))
    spreads = {'L0_xattn_bq': (0.0, 0.8),
     'L0_xattn_bk': (0.0, 0.8),
     'L0_xattn_bv': (0.0, 0.1),
     'L0_xattn_bo': (0.0, 0.1),
     'L0_ffn_router_b': (0.0, 0.1),
     'L0_ffn_expert_b': (0.0, 0.1)}
    factors = {'L0_xattn_Wq': 3.339, 'L0_xattn_Wk': 3.221}
    for name, (base, spread) in spreads.items():
        noise = np.random.default_rng([zlib.crc32(name.encode()), seed]).standard_normal(out[name].shape)
        drawn = base * np.exp(spread * noise) if base else spread * noise
        out[name] = jnp.asarray(drawn.astype(out[name].dtype))
    for name, factor in factors.items():
        out[name] = (out[name] * factor).astype(out[name].dtype)
    return out
```

```python
from contextlib import ExitStack

import concourse.bass as bass
from concourse import mybir

F32 = mybir.dt.float32
F32R = mybir.dt.float32r
BF16 = mybir.dt.bfloat16
U8 = mybir.dt.uint8
U32 = mybir.dt.uint32
ALU = mybir.AluOpType
ACT = mybir.ActivationFunctionType
AX_X = mybir.AxisListType.X

P = 128
BIG = float(2 ** 100)
EPS = 1e-5


def xattn_moe_kernel(nc, x, ctx_in, attn_mask, key_mask, Wq, bq, Wk, bk, Wv, bv, Wo, bo,
                     router_w, router_b, expert_w, expert_b, out):
    B, T, D = x.shape
    S = ctx_in.shape[1]
    E = router_w.shape[1]
    H = 16
    DK = D // H
    SCALE = 1.0 / float(DK) ** 0.5
    KC = D // P
    TH = T // P
    HC = H // KC
    G = 4
    NF = H // 2
    NM = TH * H // G
    NY = TH * E // 2

    es = ExitStack()
    with es:
        def sb(name, shape, dt=F32):
            return es.enter_context(nc.sbuf_tensor(name, shape, dt))

        def sem(name):
            return es.enter_context(nc.semaphore(name))

        identf = sb("identf", [P, P])
        identb = sb("identb", [P, P], BF16)
        sel = sb("sel", [P, HC, S], BF16)
        ind = sb("ind", [P, HC])
        iota8 = sb("iota8", [P, E])
        mhalf = sb("mhalf", [P, TH])
        w_nat = sb("w_nat", [P, 4, KC, D])
        wH = sb("wH", [P, 4, KC, D], F32R)
        wL = sb("wL", [P, 4, KC, D], F32R)
        e_nat = sb("e_nat", [P, KC, E, D])
        eH = sb("eH", [P, KC, E, D], F32R)
        eL = sb("eL", [P, KC, E, D], F32R)
        r_nat = sb("r_nat", [P, KC, E])
        rH = sb("rH", [P, KC, E], F32R)
        rL = sb("rL", [P, KC, E], F32R)
        bq_c = sb("bq_c", [P, KC])
        bk_c = sb("bk_c", [P, KC])
        bv_b = sb("bv_b", [P, D])
        bo_b = sb("bo_b", [P, D])
        rb_b = sb("rb_b", [P, E])
        eb = sb("eb", [E, D])
        am8 = sb("am8", [P, TH, S], U8)
        attnb = sb("attnb", [P, TH, S])
        XR = 4
        xr = sb("xr", [P, XR, TH, D])
        ctxs = sb("ctxs", [S, 2, D])
        kp8 = sb("kp8", [P, 2, S], U8)
        st1 = sb("st1", [P, TH, 6])
        mv1 = sb("mv1", [P, TH, 2])
        rs1 = sb("rs1", [P, TH])
        ve1 = sb("ve1", [P, TH])
        xn = sb("xn", [P, TH, D])
        xH = sb("xH", [P, KC, T], F32R)
        xL = sb("xL", [P, KC, T], F32R)
        qH = sb("qH", [P, 2, KC, T], F32R)
        qL = sb("qL", [P, 2, KC, T], F32R)
        cH = sb("cH", [P, KC, S], F32R)
        cL = sb("cL", [P, KC, S], F32R)
        kH = sb("kH", [P, KC, S], F32R)
        kL = sb("kL", [P, KC, S])
        kbH = sb("kbH", [P, 2, H, S], F32R)
        kbL = sb("kbL", [P, 2, H, S], F32R)
        va = sb("va", [S, 2, H, 2, DK])
        tb = sb("tb", [P, 2, TH, KC, P], BF16)
        tT = sb("tT", [P, 2, KC, T], BF16)
        mb = sb("mb", [P, TH])
        mg = sb("mg", [P, TH])
        mr = sb("mr", [P, TH])
        nanf = sb("nanf", [P, 2, TH])
        PR = 4
        pr = sb("pr", [S, PR, 2, T])
        ou = sb("ou", [P, H // G, T])
        rd = sb("rd", [P, TH, H])
        rdn = sb("rdn", [P, TH, H])
        on = sb("on", [P, TH, D])
        oH = sb("oH", [P, KC, T], F32R)
        oL = sb("oL", [P, KC, T], F32R)
        st2 = sb("st2", [P, TH, 6])
        mv2 = sb("mv2", [P, TH, 2])
        rs2 = sb("rs2", [P, TH])
        ve2 = sb("ve2", [P, TH])
        hn = sb("hn", [P, TH, D])
        hH = sb("hH", [P, 2, KC, T], F32R)
        hL = sb("hL", [P, 2, KC, T], F32R)
        lgT = sb("lgT", [E, T])
        lg = sb("lg", [P, TH, E])
        mx8 = sb("mx8", [P, TH, 8])
        ix8 = sb("ix8", [P, TH, 8], U32)
        ixf = sb("ixf", [P, TH])
        lc = sb("lc", [P, TH, E])
        le = sb("le", [P, TH, E])
        sm = sb("sm", [P, TH])
        gt = sb("gt", [P, TH])
        dsp = sb("dsp", [P, 2, TH, E])
        dT = sb("dT", [E, T])

        ps = [es.enter_context(nc.psum_tensor(f"ps{i}", [P, 512], F32)) for i in range(8)]
        TR, PJ, OV = ps[0], ps[1], ps[7]
        MX = [ps[2], ps[3]]
        ST = [ps[4], ps[5], ps[6]]
        TRk = TR[:, :].rearrange("p (k t) -> p k t", k=KC)
        PJk = PJ[:, :].rearrange("p (k t) -> p k t", k=KC)
        OVg = OV[:, :].rearrange("p (g t) -> p g t", g=2)

        S_ = {}

        def s(name):
            if name not in S_:
                S_[name] = sem(name)
            return S_[name]

        for n in ("d_w d_e d_bias d_x0 d_x1 d_x2 d_x3 d_c0 d_c1 d_k0 d_k1 d_o0 d_o1 d_o2 d_o3 "
                  "c_pool c_dve p_w a_w v_w a_e v_e "
                  "g_r1 g_r2 p_xT p_q p_cT p_k p_v p_st p_pv p_mx p_T p_ot p_on p_op p_hT p_lg p_lt p_dT p_bs p_y "
                  "a_xH a_qH a_cH a_kH a_kb a_exp a_onH a_hH a_lg a_le "
                  "v_ve1 v_xn v_xL v_qL v_cL v_kL v_kbL v_va v_tb v_mx v_T v_ov v_on v_rd v_onL v_x1 v_ve2 v_hn v_hL v_lc v_lg v_dsp v_dT v_acc v_y "
                  "dve").split():
            s(n)

        block = es.enter_context(nc.Block())

        def bc(ap, n):
            return ap.partition_broadcast(n)

        ITER = range(-1, B + 1)

        def store(sp, b):
            sp.wait_ge(s("v_y"), NY * (b + 1))
            sp.dma_start(out[b].rearrange("(h p) d -> p h d", p=P), xr[:, b % XR, :, :]).then_inc(s(f"d_o{b % XR}"), 16)

        @block.sync
        def _(sp):
            sp.dma_start(am8[:, :, :], attn_mask.rearrange("(h p) s -> p h s", p=P)).then_inc(s("d_bias"), 16)

            def load(b):
                if b >= XR:
                    sp.wait_ge(s(f"d_o{b % XR}"), 16 * (b // XR))
                sp.dma_start(xr[:, b % XR, :, :], x[b].rearrange("(h p) d -> p h d", p=P)).then_inc(s(f"d_x{b % XR}"), 16)
                if b >= 2:
                    sp.wait_ge(s("p_cT"), b - 1)
                sp.dma_start(ctxs[:, b % 2, :], ctx_in[b]).then_inc(s(f"d_c{b % 2}"), 16)
                if b >= 2:
                    sp.wait_ge(s("v_tb"), b - 1)
                sp.dma_start(kp8[:, b % 2, :], key_mask[b].partition_broadcast(P)).then_inc(s(f"d_k{b % 2}"), 16)

            load(0)
            for i, w in enumerate((Wq, Wk, Wv, Wo)):
                sp.dma_start(w_nat[:, i, :, :], w.rearrange("(k p) d -> p k d", p=P)).then_inc(s("d_w"), 16)
            sp.dma_start(bq_c[:, :], bq.rearrange("(m p) -> p m", p=P), allow_slow_non_contiguous=True).then_inc(s("d_bias"), 16)
            sp.dma_start(bk_c[:, :], bk.rearrange("(m p) -> p m", p=P), allow_slow_non_contiguous=True).then_inc(s("d_bias"), 16)
            sp.dma_start(bv_b[:, :], bv.partition_broadcast(P)).then_inc(s("d_bias"), 16)
            sp.dma_start(bo_b[:, :], bo.partition_broadcast(P)).then_inc(s("d_bias"), 16)
            sp.dma_start(rb_b[:, :], router_b.partition_broadcast(P)).then_inc(s("d_bias"), 16)
            sp.dma_start(eb[:, :], expert_b).then_inc(s("d_bias"), 16)
            sp.dma_start(r_nat[:, :, :], router_w.rearrange("(k p) e -> p k e", p=P)).then_inc(s("d_bias"), 16)
            load(1)
            for k in range(KC):
                sp.dma_start(e_nat[:, k, :, :], expert_w.rearrange("e (k p) d -> k p e d", p=P)[k]).then_inc(s("d_e"), 16)
            for b in range(B):
                if b >= 2:
                    store(sp, b - 2)
                if b + 2 < B:
                    load(b + 2)
            store(sp, B - 2)
            store(sp, B - 1)
            for i in range(XR):
                sp.wait_ge(s(f"d_o{i}"), 16 * (B // XR))

        NPOOL = 0

        @block.gpsimd
        def _(pool):
            c = s("c_pool")
            pool.memset(identf[:, :], 0.0).then_inc(c, 1)
            pool.memset(identb[:, :], 0.0).then_inc(c, 1)
            pool.memset(sel[:, :, :], 0.0).then_inc(c, 1)
            pool.memset(ind[:, :], 1.0).then_inc(c, 1)
            pool.memset(mhalf[:, :], -0.5).then_inc(c, 1)
            pool.iota(iota8[:, :], pattern=[[1, E]], base=0, channel_multiplier=0,
                      allow_small_or_imprecise_dtypes=True).then_inc(c, 1)
            pool.wait_ge(c, 6)
            for m in (identf, identb):
                pool.affine_select(out=m[:, :], in_=m[:, :], compare_op=ALU.not_equal, fill=1.0,
                                   base=0, pattern=[[-1, P]], channel_multiplier=1).then_inc(c, 1)
            pool.affine_select(out=sel[:, :, :], in_=sel[:, :, :], compare_op=ALU.not_equal, fill=1.0,
                               base=0, pattern=[[0, HC], [-1, S]], channel_multiplier=1).then_inc(c, 1)
            pool.affine_select(out=ind[:, :], in_=ind[:, :], compare_op=ALU.is_ge, fill=0.0,
                               base=0, pattern=[[-DK, HC]], channel_multiplier=1).then_inc(c, 1)
            pool.wait_ge(c, 10)
            pool.affine_select(out=sel[:, :, :], in_=sel[:, :, :], compare_op=ALU.not_equal, fill=1.0,
                               base=-S, pattern=[[-1, HC], [0, S]], channel_multiplier=1).then_inc(c, 1)
            pool.affine_select(out=ind[:, :], in_=ind[:, :], compare_op=ALU.is_ge, fill=0.0,
                               base=DK - 1, pattern=[[DK, HC]], channel_multiplier=-1).then_inc(c, 1)
            pool.wait_ge(c, 12)
            for b in ITER:
                if b + 1 < B:
                    pool.wait_ge(s("v_ve1"), b + 2)
                    if b >= 0:
                        pool.wait_ge(s("v_xn"), b + 1)
                    pool.tensor_tensor(rs1[:, :], ve1[:, :], mhalf[:, :], ALU.pow).then_inc(s("g_r1"), 1)
                if 0 <= b < B:
                    pool.wait_ge(s("v_ve2"), b + 1)
                    if b >= 1:
                        pool.wait_ge(s("v_hn"), b)
                    pool.tensor_tensor(rs2[:, :], ve2[:, :], mhalf[:, :], ALU.pow).then_inc(s("g_r2"), 1)

        @block.tensor
        def _(pe):
            pe.wait_ge(s("c_pool"), 12)
            wb = [MX[0], MX[1], ST[0], ST[1]]
            for i in range(4):
                pe.wait_ge(s("d_w"), 64)
                for kin in range(KC):
                    for ko in range(KC):
                        t = pe.transpose(wb[i][:, kin * D + ko * P:kin * D + (ko + 1) * P],
                                         w_nat[:, i, ko, kin * P:(kin + 1) * P], identf[:, :])
                t.then_inc(s("p_w"), 1)

            def three(out_ap, l, r, last, first=True):
                n = 0
                for k in range(KC):
                    for a, c in ((l[0], r[0]), (l[0], r[1]), (l[1], r[0])):
                        n += 1
                        t = pe.matmul(out_ap, a(k), c(k), start=(n == 1), stop=(n == 3 * KC))
                return t

            def a1(b):
                pe.wait_ge(s("v_xn"), b + 1)
                if b >= 1:
                    pe.wait_ge(s("v_va"), b)
                pe.wait_ge(s("v_hL"), max(b - 1, 0)) if b >= 2 else None
                for k in range(KC):
                    for h in range(TH):
                        t = pe.transpose(TRk[:, k, h * P:(h + 1) * P], xn[:, h, k * P:(k + 1) * P], identf[:, :])
                t.then_inc(s("p_xT"), 1)

            def a2(b):
                pe.wait_ge(s("v_xL"), b + 1)
                for m in range(KC):
                    t = three(PJk[:, m, :],
                              (lambda k: wH[:, 0, k, m * P:(m + 1) * P], lambda k: wL[:, 0, k, m * P:(m + 1) * P]),
                              (lambda k: xH[:, k, :], lambda k: xL[:, k, :]), False)
                t.then_inc(s("p_q"), 1)

            def a3(b):
                pe.wait_ge(s(f"d_c{b % 2}"), 16 * (b // 2 + 1))
                for k in range(KC):
                    t = pe.transpose(TR[:, k * S:(k + 1) * S], ctxs[:, b % 2, k * P:(k + 1) * P], identf[0:S, 0:S])
                t.then_inc(s("p_cT"), 1)

            def a4(b):
                pe.wait_ge(s("v_cL"), b + 1)
                pe.wait_ge(s("v_qL"), b + 1)
                for m in range(KC):
                    t = three(PJ[:, m * S:(m + 1) * S],
                              (lambda k: wH[:, 1, k, m * P:(m + 1) * P], lambda k: wL[:, 1, k, m * P:(m + 1) * P]),
                              (lambda k: cH[:, k, :], lambda k: cL[:, k, :]), False)
                t.then_inc(s("p_k"), 1)

            def a5(b):
                t = three(TR[0:S, 0:D], (lambda k: cH[:, k, :], lambda k: cL[:, k, :]),
                          (lambda k: wH[:, 2, k, :], lambda k: wL[:, 2, k, :]), False)
                t.then_inc(s("p_v"), 1)

            def mx(b, i):
                h, c, q = i // 4, (i // 2) % 2, i % 2
                if i == 0:
                    pe.wait_ge(s("a_kb"), b + 1)
                    pe.wait_ge(s("v_tb"), b + 1)
                n = NM * b + i
                if n >= 2:
                    pe.wait_ge(s("v_mx"), n - 1)
                o = MX[i % 2][:, 0:G * S]
                hd = c * HC + q * G
                pe.matmul(o, qH[:, b % 2, c, h * P:(h + 1) * P], kbH[:, b % 2, hd:hd + G, :], start=True, stop=False)
                pe.matmul(o, identb[:, :], tb[:, b % 2, h, c, 0:S].unsqueeze(1).to_broadcast([P, G, S]),
                          start=False, stop=True).then_inc(s("p_mx"), 1)

            def turn_T(b):
                pe.wait_ge(s("v_mx"), NM * (b + 1))
                TRb = TR[:, 0:KC * T // 2].bitcast(BF16).rearrange("p (c t) -> p c t", c=KC)
                for c in range(KC):
                    for h in range(TH):
                        t = pe.transpose(TRb[:, c, h * P:(h + 1) * P], tb[:, b % 2, h, c, :], identb[:, :])
                t.then_inc(s("p_T"), 1)

            def st(b, f):
                n = NF * b + f
                if f == 0:
                    pe.wait_ge(s("v_T"), b + 1)
                    pe.wait_ge(s("v_kbL"), b + 1)
                    if b >= 2:
                        pe.wait_ge(s("v_y"), NY * (b - 1))
                if n >= 3:
                    pe.wait_ge(s("a_exp"), n - 2)
                for j in range(2):
                    hd = 2 * f + j
                    c = hd // HC
                    o = ST[f % 3][0:S, j * T:(j + 1) * T]
                    pe.matmul(o, kbH[:, b % 2, hd, :], qH[:, b % 2, c, :], start=True, stop=False)
                    pe.matmul(o, kbL[:, b % 2, hd, :], qH[:, b % 2, c, :], start=False, stop=False)
                    pe.matmul(o, kbH[:, b % 2, hd, :], qL[:, b % 2, c, :], start=False, stop=False)
                    t = pe.matmul(o, sel[:, hd % HC, :], tT[:, b % 2, c, :], start=False, stop=True)
                t.then_inc(s("p_st"), 1)

            def pv(b, g):
                pe.wait_ge(s("a_exp"), NF * b + 2 * g + 2)
                pe.wait_ge(s("v_va"), b + 1)
                if g % 2 == 0 and (b or g):
                    pe.wait_ge(s("v_ov"), 2 * b + g // 2)
                for j in range(G):
                    hd = G * g + j
                    t = pe.matmul(OVg[32 * j:32 * j + 32, g % 2, :], va[:, b % 2, hd, :, :],
                                  pr[:, (hd // 2) % PR, hd % 2, :], start=True, stop=True)
                t.then_inc(s("p_pv"), 1)

            def c1(b):
                pe.wait_ge(s("v_ov"), 2 * b + 2)
                if b + 1 < B:
                    pe.wait_ge(s("v_va"), b + 2)
                    pe.wait_ge(s("v_kL"), b + 2)
                if b >= 1:
                    pe.wait_ge(s("v_acc"), b)
                for h, bank in enumerate((TR, PJ)):
                    for g in range(H // G):
                        t = pe.transpose(bank[:, g * P:(g + 1) * P], ou[:, g, h * P:(h + 1) * P], identf[:, :])
                    t.then_inc(s("p_ot"), 1)

            def c2(b):
                pe.wait_ge(s("v_on"), TH * (b + 1))
                for k in range(KC):
                    for h in range(TH):
                        t = pe.transpose(TRk[:, k, h * P:(h + 1) * P], on[:, h, k * P:(k + 1) * P], identf[:, :])
                t.then_inc(s("p_on"), 1)

            def c3(b):
                pe.wait_ge(s("v_onL"), b + 1)
                for h in range(TH):
                    t = three(PJk[:, h, :],
                              (lambda k: oH[:, k, h * P:(h + 1) * P], lambda k: oL[:, k, h * P:(h + 1) * P]),
                              (lambda k: wH[:, 3, k, :], lambda k: wL[:, 3, k, :]), False)
                t.then_inc(s("p_op"), 1)

            def c4(b):
                pe.wait_ge(s("v_hn"), b + 1)
                for k in range(KC):
                    for h in range(TH):
                        t = pe.transpose(TRk[:, k, h * P:(h + 1) * P], hn[:, h, k * P:(k + 1) * P], identf[:, :])
                t.then_inc(s("p_hT"), 1)

            def c5(b):
                pe.wait_ge(s("v_hL"), b + 1)
                t = three(PJ[0:E, 0:T], (lambda k: rH[:, k, :], lambda k: rL[:, k, :]),
                          (lambda k: hH[:, b % 2, k, :], lambda k: hL[:, b % 2, k, :]), False)
                t.then_inc(s("p_lg"), 1)

            def c6(b):
                pe.wait_ge(s("a_lg"), b + 1)
                for h in range(TH):
                    t = pe.transpose(PJ[:, h * E:(h + 1) * E], lgT[:, h * P:(h + 1) * P], identf[0:E, 0:E])
                t.then_inc(s("p_lt"), 1)

            def c7(b):
                pe.wait_ge(s("v_dsp"), b + 1)
                for h in range(TH):
                    t = pe.transpose(PJ[0:E, h * P:(h + 1) * P], dsp[:, b % 2, h, :], identf[:, :])
                t.then_inc(s("p_dT"), 1)

            def c8(b, after_q):
                pe.wait_ge(s("v_dT"), b + 1)
                if after_q:
                    pe.wait_ge(s("v_qL"), b + 3)
                for h in range(TH):
                    t = pe.matmul(PJk[:, h, :], dT[:, h * P:(h + 1) * P], eb[:, :], start=True, stop=True)
                t.then_inc(s("p_bs"), 1)

            def moe(b, i):
                h, g = i // 4, i % 4
                n = NY * b + i
                if n >= 3:
                    pe.wait_ge(s("v_y"), n - 2)
                if i == 0:
                    if b + 2 <= B:
                        pe.wait_ge(s("a_exp"), NF * min(b + 2, B))
                    pe.wait_ge(s("v_acc"), b + 1)
                t = three(ST[i % 3][:, :],
                          (lambda k: hH[:, b % 2, k, h * P:(h + 1) * P], lambda k: hL[:, b % 2, k, h * P:(h + 1) * P]),
                          (lambda k: eH[:, k, 2 * g:2 * g + 2, :], lambda k: eL[:, k, 2 * g:2 * g + 2, :]), False)
                t.then_inc(s("p_y"), 1)

            for b in ITER:
                cur, nxt, prv = 0 <= b < B, b + 1 < B, b >= 1
                for f in range(NF):
                    if cur:
                        st(b, f)
                    if f == 0 and prv:
                        c6(b - 1)
                    if f == 1 and nxt:
                        if b == -1:
                            pe.wait_ge(s("v_w"), 4)
                        a1(b + 1)
                    if f == 2 and prv:
                        c7(b - 1)
                    if f == 3 and nxt:
                        if prv:
                            pe.wait_ge(s("v_dT"), b)
                        elif b == 0:
                            pass
                        a2(b + 1)
                    if f == 4 and nxt:
                        a3(b + 1)
                    if f == 5 and prv:
                        c8(b - 1, nxt)
                    if f == 6 and nxt:
                        if prv:
                            pe.wait_ge(s("v_acc"), b)
                        a4(b + 1)
                        a5(b + 1)
                    if cur and f >= 3 and f % 2:
                        pv(b, (f - 3) // 2)
                if cur:
                    pv(b, H // G - 1)
                if prv and b == 1:
                    pe.wait_ge(s("v_e"), KC)
                for i in range(NM):
                    if nxt:
                        mx(b + 1, i)
                    if prv and i < NY - 1:
                        moe(b - 1, i)
                    if cur:
                        if i == 0:
                            c1(b)
                        if i == 2:
                            c2(b)
                        if i == 3:
                            c3(b)
                        if i == 6:
                            c4(b)
                if prv:
                    moe(b - 1, NY - 1)
                if nxt:
                    if cur:
                        pe.wait_ge(s("v_hL"), b + 1)
                    else:
                        pe.wait_ge(s("v_va"), 1)
                    turn_T(b + 1)
                if cur:
                    if b == 0:
                        pe.wait_ge(s("v_e"), KC + 1)
                    c5(b)

        @block.scalar
        def _(act):
            wb = [MX[0], MX[1], ST[0], ST[1]]
            for i in range(4):
                act.wait_ge(s("p_w"), i + 1)
                act.activation(wH[:, i, :, :], wb[i][:, :], ACT.Copy).then_inc(s("a_w"), 1)

            def phase1(b):
                cur, nxt, prv = 0 <= b < B, b + 1 < B, b >= 1
                for f in range(NF):
                    if f == 1 and nxt:
                        act.wait_ge(s("p_xT"), b + 2)
                        act.activation(xH[:, :, :], TR[:, :], ACT.Copy).then_inc(s("a_xH"), 1)
                    if f == 3 and nxt:
                        act.wait_ge(s("p_q"), b + 2)
                        if b >= 1:
                            act.wait_ge(s("p_st"), NF * b)
                        for m in range(KC):
                            act.activation(qH[:, (b + 1) % 2, m, :], PJk[:, m, :], ACT.Identity,
                                           bias=bq_c[:, m:m + 1]).then_inc(s("a_qH"), 1)
                    if f == 4 and nxt:
                        act.wait_ge(s("p_cT"), b + 2)
                        if b >= 0:
                            act.wait_ge(s("p_v"), b + 1)
                        act.activation(cH[:, :, :], TR[:, 0:KC * S], ACT.Copy).then_inc(s("a_cH"), 1)
                    if f == 6 and nxt:
                        act.wait_ge(s("p_k"), b + 2)
                        if b >= 0:
                            act.wait_ge(s("v_kbL"), b + 1)
                        for m in range(KC):
                            act.activation(kH[:, m, :], PJ[:, m * S:(m + 1) * S], ACT.Identity,
                                           bias=bk_c[:, m:m + 1]).then_inc(s("a_kH"), 1)
                    if f == 0 and prv:
                        act.wait_ge(s("v_lc"), b)
                        act.activation(le[:, :, :], lc[:, :, :], ACT.Exp).then_inc(s("a_le"), 1)
                    if cur:
                        n = NF * b + f
                        act.wait_ge(s("p_st"), n + 1)
                        if n >= PR:
                            need_f = n - PR
                            bb, ff = need_f // NF, need_f % NF
                            act.wait_ge(s("p_pv"), 4 * bb + ff // 2 + 1)
                        act.activation(pr[:, f % PR, :, :], ST[f % 3][0:S, :], ACT.Exp, scale=SCALE).then_inc(s("a_exp"), 1)
                if nxt:
                    act.wait_ge(s("a_kH"), KC * (b + 2))
                    for h in range(H):
                        a = act.activation(kbH[:, (b + 1) % 2, h, :], kH[:, h // HC, :].bitcast(F32), ACT.Copy,
                                           scale=ind[:, h % HC:h % HC + 1])
                    a.then_inc(s("a_kb"), 1)

            def phase2(b):
                if 0 <= b < B:
                    act.wait_ge(s("p_on"), b + 1)
                    act.activation(oH[:, :, :], TR[:, :], ACT.Copy).then_inc(s("a_onH"), 1)
                    act.wait_ge(s("p_hT"), b + 1)
                    act.activation(hH[:, b % 2, :, :], TR[:, :], ACT.Copy).then_inc(s("a_hH"), 1)
                    act.wait_ge(s("p_lg"), b + 1)
                    act.activation(lgT[:, :], PJ[0:E, 0:T], ACT.Copy).then_inc(s("a_lg"), 1)

            act.wait_ge(s("d_bias"), 16 * 8)
            act.wait_ge(s("c_pool"), 12)
            for b in ITER:
                phase1(b)
                if b == -1:
                    act.wait_ge(s("d_e"), 16 * KC)
                    for k in range(KC):
                        act.activation(eH[:, k, :, :], e_nat[:, k, :, :], ACT.Copy).then_inc(s("a_e"), 1)
                    act.activation(rH[:, :, :], r_nat[:, :, :], ACT.Copy).then_inc(s("a_e"), 1)
                phase2(b)

        @block.vector
        def _(v):
            cnt = [0]

            def link(ins):
                cnt[0] += 1
                ins.then_inc(s("dve"), 1)
                v.wait_ge(s("dve"), cnt[0])

            v.memset(va[:, :, :, 1, :], 1.0)
            v.wait_ge(s("d_bias"), 16 * 8)
            v.tensor_scalar(attnb[:, :, :], am8[:, :, :], -BIG, None, ALU.mult).then_inc(s("c_dve"), 1)
            wb = [MX[0], MX[1], ST[0], ST[1]]

            def ln_stats(src, stt, mvt, vet, name):
                for h in range(TH):
                    i = v.bn_stats(stt[:, h, :], src(h))
                link(i)
                for h in range(TH):
                    i = v.bn_aggr(mvt[:, h, :], stt[:, h, :])
                link(i)
                v.tensor_scalar(vet[:, :], mvt[:, :, 1], EPS, None, ALU.add).then_inc(s(name), 1)

            def phase1(b):
                cur, nxt, prv = 0 <= b < B, b + 1 < B, b >= 1
                bn, pn = b + 1, (b + 1) % 2
                if nxt:
                    v.wait_ge(s(f"d_x{bn % XR}"), 16 * (bn // XR + 1))
                    if bn >= 1:
                        v.wait_ge(s("g_r1"), bn)
                    ln_stats(lambda h: xr[:, bn % XR, h, :], st1, mv1, ve1, "v_ve1")
                if b == -1:
                    for i in range(4):
                        v.wait_ge(s("a_w"), i + 1)
                        v.tensor_tensor(wL[:, i, :, :], wb[i][:, :].rearrange("p (k d) -> p k d", k=KC),
                                        wH[:, i, :, :].bitcast(F32), ALU.subtract).then_inc(s("v_w"), 1)
                if prv:
                    pb = (b - 1) % 2
                    v.wait_ge(s("p_lt"), b)
                    link(v.tensor_tensor(lg[:, :, :], PJ[:, 0:TH * E].rearrange("p (h e) -> p h e", h=TH),
                                         rb_b[:, :].unsqueeze(1).to_broadcast([P, TH, E]), ALU.add))
                    for h in range(TH):
                        i = v.max(mx8[:, h, :], lg[:, h, :])
                    link(i)
                    v.tensor_tensor(lc[:, :, :], lg[:, :, :], mx8[:, :, 0:1].to_broadcast([P, TH, E]),
                                    ALU.subtract).then_inc(s("v_lc"), 1)
                    for h in range(TH):
                        i = v.max_index(ix8[:, h, :], mx8[:, h, :], lg[:, h, :])
                    link(i)
                    link(v.tensor_copy(ixf[:, :], ix8[:, :, 0]))
                    v.wait_ge(s("a_le"), b)
                    link(v.tensor_reduce(sm[:, :], le[:, :, :], AX_X, ALU.add))
                    link(v.reciprocal(gt[:, :], sm[:, :]))
                    for h in range(TH):
                        i = v.tensor_scalar(dsp[:, pb, h, :], iota8[:, :], ixf[:, h:h + 1], gt[:, h:h + 1],
                                            ALU.is_equal, ALU.mult)
                    i.then_inc(s("v_dsp"), 1)
                if nxt:
                    v.wait_ge(s("g_r1"), bn + 1)
                    if bn >= 1:
                        v.wait_ge(s("p_xT"), bn)
                    for h in range(TH):
                        i = v.tensor_scalar(xn[:, h, :], xr[:, bn % XR, h, :], mv1[:, h, 0:1], rs1[:, h:h + 1],
                                            ALU.subtract, ALU.mult)
                    i.then_inc(s("v_xn"), 1)
                    v.wait_ge(s("v_xn"), bn + 1)
                    for h in range(TH):
                        i = v.tensor_tensor(xr[:, bn % XR, h, :], xr[:, bn % XR, h, :], bo_b[:, :], ALU.add)
                    link(i)
                    v.wait_ge(s(f"d_k{pn}"), 16 * (bn // 2 + 1))
                    if bn >= 2:
                        v.wait_ge(s("p_T"), bn - 1)
                    for c in range(KC):
                        i = v.scalar_tensor_tensor(out=tb[:, pn, :, c, 0:S],
                                                   in0=kp8[:, pn, :].unsqueeze(1).to_broadcast([P, TH, S]),
                                                   scalar=-BIG, in1=attnb[:, :, :], op0=ALU.mult, op1=ALU.add)
                    i.then_inc(s("v_tb"), 1)
                    v.wait_ge(s("v_tb"), bn + 1)
                    link(v.tensor_reduce(mb[:, :], tb[:, pn, :, 0, 0:S], AX_X, ALU.max))
                    link(v.tensor_scalar(mg[:, :], mb[:, :], -1.0, None, ALU.is_ge))
                    link(v.reciprocal(mr[:, :], mg[:, :]))
                    link(v.tensor_tensor(nanf[:, pn, :], mg[:, :], mr[:, :], ALU.mult))
                    v.wait_ge(s("a_xH"), bn + 1)
                    v.tensor_tensor(xL[:, :, :], TRk, xH[:, :, :].bitcast(F32), ALU.subtract).then_inc(s("v_xL"), 1)
                if prv:
                    v.wait_ge(s("p_dT"), b)
                    v.tensor_copy(dT[:, :], PJ[0:E, 0:T]).then_inc(s("v_dT"), 1)
                if nxt:
                    v.wait_ge(s("a_qH"), KC * (bn + 1))
                    for m in range(KC):
                        i = v.scalar_tensor_tensor(out=qL[:, pn, m, :], in0=PJk[:, m, :], scalar=bq_c[:, m:m + 1],
                                                   in1=qH[:, pn, m, :].bitcast(F32), op0=ALU.add, op1=ALU.subtract)
                    i.then_inc(s("v_qL"), 1)
                    v.wait_ge(s("a_cH"), bn + 1)
                    v.tensor_tensor(cL[:, :, :], TR[:, 0:KC * S].rearrange("p (k s) -> p k s", k=KC),
                                    cH[:, :, :].bitcast(F32), ALU.subtract).then_inc(s("v_cL"), 1)
                if prv:
                    pb = b - 1
                    v.wait_ge(s("p_bs"), b)
                    v.tensor_tensor(xr[:, pb % XR, :, :], xr[:, pb % XR, :, :], PJk, ALU.add).then_inc(s("v_acc"), 1)
                if cur:
                    v.wait_ge(s("p_pv"), 4 * b + 2)
                    if b >= 1:
                        v.wait_ge(s("p_ot"), TH * b)
                    v.tensor_copy(ou[:, 0:2, :], OVg).then_inc(s("v_ov"), 1)
                if nxt:
                    v.wait_ge(s("a_kH"), KC * (bn + 1))
                    for m in range(KC):
                        i = v.scalar_tensor_tensor(out=kL[:, m, :], in0=PJ[:, m * S:(m + 1) * S],
                                                   scalar=bk_c[:, m:m + 1], in1=kH[:, m, :].bitcast(F32),
                                                   op0=ALU.add, op1=ALU.subtract)
                    i.then_inc(s("v_kL"), 1)
                    v.wait_ge(s("p_v"), bn + 1)
                    v.tensor_tensor(va[:, pn, :, 0, :], TR[0:S, 0:D].rearrange("p (h d) -> p h d", h=H),
                                    bv_b[0:S, :].rearrange("p (h d) -> p h d", h=H), ALU.add).then_inc(s("v_va"), 1)
                    v.wait_ge(s("v_kL"), bn + 1)
                    for m in range(KC):
                        i = v.tensor_tensor(kbL[:, pn, m * HC:(m + 1) * HC, :],
                                            kL[:, m, :].unsqueeze(1).to_broadcast([P, HC, S]),
                                            ind[:, :].unsqueeze(2).to_broadcast([P, HC, S]), ALU.mult)
                    i.then_inc(s("v_kbL"), 1)
                if cur:
                    v.wait_ge(s("p_pv"), 4 * b + 4)
                    v.tensor_copy(ou[:, 2:4, :], OVg).then_inc(s("v_ov"), 1)

            def phase2(b):
                cur, nxt, prv = 0 <= b < B, b + 1 < B, b >= 1
                bn, pn = b + 1, (b + 1) % 2

                def ymix(i):
                    bp = b - 1
                    h, g = i // 4, i % 4
                    v.wait_ge(s("p_y"), NY * bp + i + 1)
                    a = xr[:, bp % XR, h, :]
                    for j in range(2):
                        e = 2 * g + j
                        ins = v.scalar_tensor_tensor(out=a, in0=ST[i % 3][:, j * D:(j + 1) * D],
                                                     scalar=dsp[:, bp % 2, h, e:e + 1], in1=a,
                                                     op0=ALU.mult, op1=ALU.add)
                        if j == 0:
                            link(ins)
                    ins.then_inc(s("v_y"), 1)
                    v.wait_ge(s("v_y"), NY * bp + i + 1)

                for i in range(NM):
                    if nxt:
                        h, c, q = i // 4, (i // 2) % 2, i % 2
                        v.wait_ge(s("p_mx"), NM * bn + i + 1)
                        v.tensor_reduce(tb[:, pn, h, c, S + q * G:S + (q + 1) * G],
                                        MX[i % 2][:, 0:G * S].rearrange("p (g s) -> p g s", g=G),
                                        AX_X, ALU.max, negate=True).then_inc(s("v_mx"), 1)
                    if prv and i < NY - 1:
                        ymix(i)
                    if cur:
                        if i == 0:
                            for h, bank in enumerate((TR, PJ)):
                                v.wait_ge(s("p_ot"), TH * b + h + 1)
                                o4 = bank[:, :].rearrange("p (n z d) -> p n z d", n=H, z=2)
                                link(v.reciprocal(rd[:, h, :], o4[:, :, 1, 0]))
                                link(v.tensor_scalar(rdn[:, h, :], rd[:, h, :], nanf[:, b % 2, h:h + 1], None, ALU.mult))
                                v.tensor_tensor(on[:, h, :].rearrange("p (n d) -> p n d", n=H), o4[:, :, 0, :],
                                                rdn[:, h, :].unsqueeze(2).to_broadcast([P, H, DK]),
                                                ALU.mult).then_inc(s("v_on"), 1)
                        if i == 2:
                            v.wait_ge(s("a_onH"), b + 1)
                            v.tensor_tensor(oL[:, :, :], TRk, oH[:, :, :].bitcast(F32), ALU.subtract).then_inc(s("v_onL"), 1)
                        if i == 3:
                            v.wait_ge(s("p_op"), b + 1)
                            v.tensor_tensor(xr[:, b % XR, :, :], xr[:, b % XR, :, :], PJk, ALU.add).then_inc(s("v_x1"), 1)
                            v.wait_ge(s("v_x1"), b + 1)
                            ln_stats(lambda h: xr[:, b % XR, h, :], st2, mv2, ve2, "v_ve2")
                        if i == 5:
                            v.wait_ge(s("g_r2"), b + 1)
                            for h in range(TH):
                                ins = v.tensor_scalar(hn[:, h, :], xr[:, b % XR, h, :], mv2[:, h, 0:1], rs2[:, h:h + 1],
                                                      ALU.subtract, ALU.mult)
                            ins.then_inc(s("v_hn"), 1)
                        if i == 6:
                            v.wait_ge(s("a_hH"), b + 1)
                            v.tensor_tensor(hL[:, b % 2, :, :], TRk, hH[:, b % 2, :, :].bitcast(F32),
                                            ALU.subtract).then_inc(s("v_hL"), 1)
                if prv:
                    ymix(NY - 1)
                if nxt:
                    v.wait_ge(s("p_T"), bn + 1)
                    TRb = TR[:, 0:KC * T // 2].bitcast(BF16).rearrange("p (c t) -> p c t", c=KC)
                    v.tensor_copy(tT[:, pn, :, :], TRb).then_inc(s("v_T"), 1)

            for b in ITER:
                phase1(b)
                if b == -1:
                    for k in range(KC):
                        v.wait_ge(s("a_e"), k + 1)
                        v.tensor_tensor(eL[:, k, :, :], e_nat[:, k, :, :], eH[:, k, :, :].bitcast(F32),
                                        ALU.subtract).then_inc(s("v_e"), 1)
                    v.wait_ge(s("a_e"), KC + 1)
                    v.tensor_tensor(rL[:, :, :], r_nat[:, :, :], rH[:, :, :].bitcast(F32), ALU.subtract).then_inc(s("v_e"), 1)
                phase2(b)


_INS = ['x', 'ctx_1024', 'mask_SxS2_bk1', 'mask_BxS2_bf0', 'L0_xattn_Wq', 'L0_xattn_bq', 'L0_xattn_Wk',
        'L0_xattn_bk', 'L0_xattn_Wv', 'L0_xattn_bv', 'L0_xattn_Wo', 'L0_xattn_bo', 'L0_ffn_router_w',
        'L0_ffn_router_b', 'L0_ffn_expert_w', 'L0_ffn_expert_b']
_OUTS = [((8, 256, 256), 'float32')]


def kernel(**inputs):
    import numpy as _np
    import concourse.bacc as _bacc
    from concourse import mybir as _mybir
    from concourse.bass_utils import run_bass_kernel_spmd as _run

    nc = _bacc.Bacc("TRN2", target_bir_lowering=False, num_devices=1)
    arrays, args = {}, []
    for name in _INS:
        a = _np.ascontiguousarray(inputs[name])
        arrays[f"in_{name}_dram"] = a
        args.append(nc.dram_tensor(f"in_{name}_dram", a.shape, _mybir.dt.from_np(a.dtype), kind="ExternalInput").ap())
    for i, (shape, dtype) in enumerate(_OUTS):
        dt = _mybir.dt.from_np(_np.dtype(dtype))
        args.append(nc.dram_tensor(f"out_{i}_dram", shape, dt, kind="ExternalOutput").ap())
    xattn_moe_kernel(nc, *args)
    r = _run(nc, [arrays], core_ids=[0])
    return r.results[0]["out_0_dram"]
```

```python
from contextlib import ExitStack

import concourse.bass as bass
from concourse import mybir

F32 = mybir.dt.float32
F32R = mybir.dt.float32r
BF16 = mybir.dt.bfloat16
U8 = mybir.dt.uint8
U32 = mybir.dt.uint32
ALU = mybir.AluOpType
ACT = mybir.ActivationFunctionType
AX_X = mybir.AxisListType.X

P = 128
BIG = float(2 ** 100)
EPS = 1e-5


def xattn_moe_kernel(nc, x, ctx_in, attn_mask, key_mask, Wq, bq, Wk, bk, Wv, bv, Wo, bo,
                     router_w, router_b, expert_w, expert_b, out):
    B, T, D = x.shape
    S = ctx_in.shape[1]
    E = router_w.shape[1]
    H = 16
    DK = D // H
    SCALE = 1.0 / float(DK) ** 0.5
    KC = D // P
    TH = T // P
    HC = H // KC
    G = 4
    NF = H // 2
    NM = TH * H // G
    NT = B * TH
    SB = B - 2
    NS = SB * TH
    NB = NS + E - 1
    EP = E // 2
    NU = TH * EP
    HR = 4

    es = ExitStack()
    scr_h = nc.dram_tensor("sorted_h", [NB * P, D], F32).ap()
    scr_y = nc.dram_tensor("sorted_y", [NB * P, D], F32).ap()
    with es:
        def sb(name, shape, dt=F32):
            return es.enter_context(nc.sbuf_tensor(name, shape, dt))

        def sem(name):
            return es.enter_context(nc.semaphore(name))

        identf = sb("identf", [P, P])
        identb = sb("identb", [P, P], BF16)
        sel = sb("sel", [P, HC, S], BF16)
        ind = sb("ind", [P, HC])
        iota8 = sb("iota8", [P, E])
        mhalf = sb("mhalf", [P, TH])
        w_nat = sb("w_nat", [P, 4, KC, D])
        wH = sb("wH", [P, 4, KC, D], F32R)
        wL = sb("wL", [P, 4, KC, D], F32R)
        e_nat = sb("e_nat", [P, E, D])
        eH = sb("eH", [P, KC, E, D], F32R)
        eL = sb("eL", [P, KC, E, D], F32R)
        r_nat = sb("r_nat", [P, KC, E])
        rH = sb("rH", [P, KC, E], F32R)
        rL = sb("rL", [P, KC, E], F32R)
        bq_c = sb("bq_c", [P, KC])
        bk_c = sb("bk_c", [P, KC])
        bv_b = sb("bv_b", [P, D])
        bo_b = sb("bo_b", [P, D])
        rb_b = sb("rb_b", [P, E])
        eb = sb("eb", [E, D])
        am8 = sb("am8", [P, TH, S], U8)
        attnb = sb("attnb", [P, TH, S])
        XR = B
        xr = sb("xr", [P, XR, TH, D])
        ctxs = sb("ctxs", [S, 2, D])
        kp8 = sb("kp8", [P, 2, S], U8)
        st1 = sb("st1", [P, TH, 6])
        mv1 = sb("mv1", [P, TH, 2])
        rs1 = sb("rs1", [P, TH])
        ve1 = sb("ve1", [P, TH])
        xn = sb("xn", [P, TH, D])
        xH = sb("xH", [P, KC, T], F32R)
        xL = sb("xL", [P, KC, T], F32R)
        qH = sb("qH", [P, 3, KC, T], F32R)
        qL = sb("qL", [P, 3, KC, T], F32R)
        cH = sb("cH", [P, KC, S], F32R)
        cL = sb("cL", [P, KC, S], F32R)
        kH = sb("kH", [P, KC, S], F32R)
        kL = sb("kL", [P, 2, KC, S])
        kbH = sb("kbH", [P, 3, H, S], F32R)
        kbL = sb("kbL", [P, 2, H, S], F32R)
        va = sb("va", [S, 3, H, 2, DK])
        tb = sb("tb", [P, 2, TH, KC, P], BF16)
        tT = sb("tT", [P, 2, KC, T], BF16)
        mb = sb("mb", [P, TH])
        mg = sb("mg", [P, TH])
        mr = sb("mr", [P, TH])
        nanf = sb("nanf", [P, 4, TH])
        PR = 4
        assert PR * 2 * T == 4 * KC * D
        pr = w_nat[0:S, :, :, :].rearrange("p w k d -> p (w k d)").rearrange(
            "p (r j t) -> p r j t", r=PR, j=2)
        ou = sb("ou", [P, H // G, T])
        rd = sb("rd", [P, TH, H])
        rdn = sb("rdn", [P, TH, H])
        on = sb("on", [P, TH, D])
        oH = sb("oH", [P, KC, T], F32R)
        oL = sb("oL", [P, KC, T], F32R)
        st2 = sb("st2", [P, TH, 6])
        mv2 = sb("mv2", [P, TH, 2])
        rs2 = sb("rs2", [P, TH])
        ve2 = sb("ve2", [P, TH])
        hn = sb("hn", [P, NT, D])
        hH = sb("hH", [P, KC, T], F32R)
        hL = sb("hL", [P, KC, T], F32R)
        utri = sb("utri", [P, P], BF16)
        onesb = sb("onesb", [P, P], BF16)
        tri8 = sb("tri8", [P, E, E])
        j128 = sb("j128", [P, NS])
        jblk = sb("jblk", [P, NB])
        zer = sb("zer", [P, D])
        oh = sb("oh", [P, NT, E], BF16)
        cum = sb("cum", [P, NS + 1, E], BF16)
        gts = sb("gts", [P, NT])
        tot = sb("tot", [P, E])
        cmpn = sb("cmpn", [P, E, NS])
        nblk = sb("nblk", [P, E])
        trin = sb("trin", [P, E, E])
        sbk = sb("sbk", [P, E])
        endb = sb("endb", [P, E])
        base = sb("base", [P, E])
        rk = sb("rk", [P, NS, E])
        rk2 = sb("rk2", [P, NS, E])
        slotf = sb("slotf", [P, NS])
        slot = sb("slot", [P, NS], U32)
        cmpb = sb("cmpb", [P, NB, E])
        bef = sb("bef", [P, NB])
        be = sb("be", [P, NB], mybir.dt.int32)
        hb, yb = e_nat[:, 0:HR, :], e_nat[:, HR:2 * HR, :]
        bH = sb("bH", [P, 2, KC, P], F32R)
        bL = sb("bL", [P, 2, KC, P], F32R)
        gy = hn
        lgT = sb("lgT", [E, T])
        lg = sb("lg", [P, TH, E])
        mx8 = sb("mx8", [P, TH, 8])
        ix8 = sb("ix8", [P, TH, 8], U32)
        ixf = sb("ixf", [P, TH])
        lc = sb("lc", [P, TH, E])
        le = sb("le", [P, TH, E])
        sm = sb("sm", [P, TH])
        dsp = sb("dsp", [P, 2, TH, E])
        dT = sb("dT", [E, T])

        ps = [es.enter_context(nc.psum_tensor(f"ps{i}", [P, 512], F32)) for i in range(8)]
        TR, PJ, OV = ps[0], ps[1], ps[7]
        MX = [ps[2], ps[3]]
        ST = [ps[4], ps[5]]
        RT = ps[6]
        RTk = RT[:, :].rearrange("p (k t) -> p k t", k=KC)
        TRk = TR[:, :].rearrange("p (k t) -> p k t", k=KC)
        PJk = PJ[:, :].rearrange("p (k t) -> p k t", k=KC)
        OVg = OV[:, :].rearrange("p (g t) -> p g t", g=2)

        WB = [MX[0], MX[1], ST[0], ST[1]]

        S_ = {}

        def s(name):
            if name not in S_:
                S_[name] = sem(name)
            return S_[name]

        for n in ("d_w d_e d_bias d_z d_c0 d_c1 d_k0 d_k1 d_out d_sc "
                  "c_pool c_dve p_w p_dn v_dn a_T a_dT a_w v_w a_e v_e "
                  "g_r1 g_r2 p_xT p_q p_cT p_k p_v p_st p_pv p_mx p_T p_ot p_on p_op p_hT p_lg p_lt p_dT p_bs p_y "
                  "a_xH a_qH a_cH a_kH a_kb a_exp a_onH a_hH a_lg a_le "
                  "v_ve1 v_xn v_xL v_qL v_cL v_kL v_kbL v_va v_tb v_mx v_ov v_on v_rd v_onL v_x1 v_ve2 v_hn v_hL v_lc v_lg v_dsp v_acc v_y "
                  "a_ov g_xbo v_cum v_rk a_r v_r p_rk v_be v_idx p_bT a_bH v_bL p_by a_y v_fin "
                  "dve").split() + [f"d_x{b}" for b in range(B)] + [f"d_hb{i}" for i in range(HR)] + [f"d_gy{i}" for i in range(NS)] + [f"d_ys{i}" for i in range(HR)]:
            s(n)

        block = es.enter_context(nc.Block())

        ITER = range(-2, B + 2)
        MAXIMA = [[0, 1], [2], [3], [4], [5], [6], [7], []]

        def hidden_buf(b):
            return (xH, xL) if b == B - 1 else (hH, hL)

        def unit(u):
            b, n = SB + u // NU, u % NU
            return b, n // TH, n % TH, (ST[0], ST[1], MX[0], MX[1])[u % 4]

        TURN = [MX[0][:, 0:D], ST[0][:, 0:D]]
        PROD = [MX[1][:, 0:D], ST[1][:, 0:D]]

        @block.sync
        def _(sp):
            def load(b):
                sp.dma_start(xr[:, b, :, :], x[b].rearrange("(h p) d -> p h d", p=P)).then_inc(s(f"d_x{b}"), 16)
                if b >= 2:
                    sp.wait_ge(s("p_cT"), b - 1)
                sp.dma_start(ctxs[:, b % 2, :], ctx_in[b]).then_inc(s(f"d_c{b % 2}"), 16)
                if b >= 2:
                    sp.wait_ge(s("v_tb"), b - 1)
                sp.dma_start(kp8[:, b % 2, :], key_mask[b].partition_broadcast(P)).then_inc(s(f"d_k{b % 2}"), 16)

            load(0)
            for i, w in enumerate((Wq, Wk, Wv, Wo)):
                sp.dma_start(w_nat[:, i, :, :], w.rearrange("(k p) d -> p k d", p=P)).then_inc(s("d_w"), 16)
            sp.dma_start(bq_c[:, :], bq.rearrange("(m p) -> p m", p=P), allow_slow_non_contiguous=True).then_inc(s("d_bias"), 16)
            sp.dma_start(bk_c[:, :], bk.rearrange("(m p) -> p m", p=P), allow_slow_non_contiguous=True).then_inc(s("d_bias"), 16)
            sp.dma_start(am8[:, :, :], attn_mask.rearrange("(h p) s -> p h s", p=P)).then_inc(s("d_bias"), 16)
            sp.dma_start(bo_b[:, :], bo.partition_broadcast(P)).then_inc(s("d_bias"), 16)
            sp.dma_start(bv_b[:, :], bv.partition_broadcast(P)).then_inc(s("d_bias"), 16)
            sp.dma_start(rb_b[:, :], router_b.partition_broadcast(P)).then_inc(s("d_bias"), 16)
            sp.dma_start(eb[:, :], expert_b).then_inc(s("d_bias"), 16)
            sp.dma_start(r_nat[:, :, :], router_w.rearrange("(k p) e -> p k e", p=P)).then_inc(s("d_bias"), 16)
            load(1)
            sp.dma_start(e_nat[:, :, :], expert_w.rearrange("e (k p) d -> k p e d", p=P)[0]).then_inc(s("d_e"), 16)
            sp.wait_ge(s("c_dve"), 3)
            sp.dma_start(scr_h.rearrange("(p n) d -> p n d", p=P),
                         zer[:, :].unsqueeze(1).to_broadcast([P, NB, D])).then_inc(s("d_z"), 16)
            load(2)
            load(3)
            sp.wait_ge(s("v_e"), 1)
            sp.dma_start(e_nat[:, :, :], expert_w.rearrange("e (k p) d -> k p e d", p=P)[1]).then_inc(s("d_e"), 16)
            for b in range(4, B):
                load(b)

            def load_block(j):
                if j >= HR:
                    sp.wait_ge(s("p_bT"), j - HR + 1)
                sp.dma_start(hb[:, j % HR, :], scr_h[j * P:(j + 1) * P, :]).then_inc(s(f"d_hb{j % HR}"), 16)

            def store_block(j):
                sp.wait_ge(s("a_y"), j + 1)
                sp.dma_start(scr_y[j * P:(j + 1) * P, :], yb[:, j % HR, :]).then_inc(s(f"d_ys{j % HR}"), 16)

            sp.wait_ge(s("v_e"), KC)
            sp.wait_ge(s("d_sc"), 16 * NS)
            for j in range(HR):
                load_block(j)
            for j in range(NB):
                if j + HR < NB:
                    load_block(j + HR)
                store_block(j)
            for t in list(range(NS, NT)) + list(range(NS)):
                if t < NS:
                    sp.wait_ge(s("v_fin"), t + 1)
                else:
                    sp.wait_ge(s("v_dn"), (t // TH - SB) * NU + (EP - 1) * TH + t % TH + 1)
                sp.dma_start(out[t // TH, (t % TH) * P:(t % TH + 1) * P, :], xr[:, t // TH, t % TH, :]).then_inc(s("d_out"), 16)
            sp.wait_ge(s("d_out"), 16 * NT)

        @block.gpsimd
        def _(pool):
            c = s("c_pool")
            pool.memset(identf[:, :], 0.0).then_inc(c, 1)
            pool.memset(identb[:, :], 0.0).then_inc(c, 1)
            pool.memset(sel[:, :, :], 0.0).then_inc(c, 1)
            pool.memset(ind[:, :], 1.0).then_inc(c, 1)
            pool.memset(mhalf[:, :], -0.5).then_inc(c, 1)
            pool.iota(iota8[:, :], pattern=[[1, E]], base=0, channel_multiplier=0,
                      allow_small_or_imprecise_dtypes=True).then_inc(c, 1)
            pool.memset(utri[:, :], 1.0).then_inc(c, 1)
            pool.memset(tri8[:, :, :], 1.0).then_inc(c, 1)
            pool.memset(onesb[:, :], 1.0).then_inc(c, 1)
            pool.iota(j128[:, :], pattern=[[P, NS]], base=0, channel_multiplier=0,
                      allow_small_or_imprecise_dtypes=True).then_inc(c, 1)
            pool.iota(jblk[:, :], pattern=[[1, NB]], base=0, channel_multiplier=0,
                      allow_small_or_imprecise_dtypes=True).then_inc(c, 1)
            pool.wait_ge(c, 11)
            for m in (identf, identb):
                pool.affine_select(out=m[:, :], in_=m[:, :], compare_op=ALU.not_equal, fill=1.0,
                                   base=0, pattern=[[-1, P]], channel_multiplier=1).then_inc(c, 1)
            pool.affine_select(out=sel[:, :, :], in_=sel[:, :, :], compare_op=ALU.not_equal, fill=1.0,
                               base=0, pattern=[[0, HC], [-1, S]], channel_multiplier=1).then_inc(c, 1)
            pool.affine_select(out=ind[:, :], in_=ind[:, :], compare_op=ALU.is_ge, fill=0.0,
                               base=0, pattern=[[-DK, HC]], channel_multiplier=1).then_inc(c, 1)
            pool.wait_ge(c, 15)
            pool.affine_select(out=sel[:, :, :], in_=sel[:, :, :], compare_op=ALU.not_equal, fill=1.0,
                               base=-S, pattern=[[-1, HC], [0, S]], channel_multiplier=1).then_inc(c, 1)
            pool.affine_select(out=ind[:, :], in_=ind[:, :], compare_op=ALU.is_ge, fill=0.0,
                               base=DK - 1, pattern=[[DK, HC]], channel_multiplier=-1).then_inc(c, 1)
            pool.affine_select(out=utri[:, :], in_=utri[:, :], compare_op=ALU.is_gt, fill=0.0,
                               base=0, pattern=[[1, P]], channel_multiplier=-1).then_inc(c, 1)
            pool.affine_select(out=tri8[:, :, :], in_=tri8[:, :, :], compare_op=ALU.is_gt, fill=0.0,
                               base=0, pattern=[[1, E], [-1, E]], channel_multiplier=0).then_inc(c, 1)

            def rsqrt1(b):
                pool.wait_ge(s("v_ve1"), b + 1)
                if b >= 1:
                    pool.wait_ge(s("v_xn"), b)
                pool.tensor_tensor(rs1[:, :], ve1[:, :], mhalf[:, :], ALU.pow).then_inc(s("g_r1"), 1)

            def add_bo(b):
                pool.wait_ge(s("v_xn"), b + 1)
                pool.tensor_tensor(xr[:, b, :, :], xr[:, b, :, :], bo_b[:, :].unsqueeze(1).to_broadcast([P, TH, D]),
                                   ALU.add).then_inc(s("g_xbo"), 1)

            def rsqrt2(b):
                pool.wait_ge(s("v_ve2"), b + 1)
                if b >= 1:
                    pool.wait_ge(s("v_hn"), b)
                pool.tensor_tensor(rs2[:, :], ve2[:, :], mhalf[:, :], ALU.pow).then_inc(s("g_r2"), 1)

            def scatter():
                pool.wait_ge(s("v_idx"), 1)
                pool.wait_ge(s("d_z"), 16)
                for t in range(NS):
                    pool.indirect_dma_start(scr_h, bass.IndirectOffsetOnAxis(ap=slot[:, t:t + 1], axis=0),
                                            hn[:, t, :], None).then_inc(s("d_sc"), 16)

            def gather():
                for i in range(HR):
                    pool.wait_ge(s(f"d_ys{i}"), 16 * len([j for j in range(NB) if j % HR == i]))
                for t in range(NS):
                    pool.indirect_dma_start(gy[:, t, :], None, scr_y,
                                            bass.IndirectOffsetOnAxis(ap=slot[:, t:t + 1], axis=0)).then_inc(s(f"d_gy{t}"), 16)

            rsqrt1(0)
            pool.wait_ge(s("d_bias"), 16 * 8)
            add_bo(0)
            for i in ITER:
                if 0 < i + 2 < B:
                    rsqrt1(i + 2)
                    add_bo(i + 2)
                if 0 <= i - 1 < B:
                    rsqrt2(i - 1)
                if i - 2 == SB - 1:
                    scatter()
            gather()

        def dense(i, f):
            if i == B:
                n = [0, 1, 2, 3, 4, 5, 6, 7, NU]
                return range(n[f], n[f + 1])
            return range(0)

        def dense_sum(i, f):
            if i == B:
                n = [0, 0, 0, 0, 0, 2, 4, 6, NU][f:f + 2]
                return range(n[0], n[1])
            return range(0)

        def steps(i, f):
            if i == B + 1:
                return range(2 * f, 2 * f + 2)
            return range(0)

        STEPS_LEFT = range(2 * NF, NB + 1)
        DENSE_LEFT = range(NU, 2 * NU)

        RTb = RT[:, 0:KC * T // 2].bitcast(BF16).rearrange("p (c t) -> p c t", c=KC)

        @block.tensor
        def _(pe):
            pe.wait_ge(s("c_pool"), 19)
            for i in range(4):
                pe.wait_ge(s("d_w"), 64)
                for kin in range(KC):
                    for ko in range(KC):
                        t = pe.transpose(WB[i][:, kin * D + ko * P:kin * D + (ko + 1) * P],
                                         w_nat[:, i, ko, kin * P:(kin + 1) * P], identf[:, :])
                t.then_inc(s("p_w"), 1)

            def three(out_ap, l, r):
                n = 0
                for k in range(KC):
                    for a, c in ((l[0], r[0]), (l[0], r[1]), (l[1], r[0])):
                        n += 1
                        t = pe.matmul(out_ap, a(k), c(k), start=(n == 1), stop=(n == 3 * KC))
                return t

            def turn4(src):
                for k in range(KC):
                    for h in range(TH):
                        t = pe.transpose(TRk[:, k, h * P:(h + 1) * P], src(h, k), identf[:, :])
                return t

            def a_ctx_turn(b):
                pe.wait_ge(s(f"d_c{b % 2}"), 16 * (b // 2 + 1))
                for k in range(KC):
                    t = pe.transpose(TR[:, k * S:(k + 1) * S], ctxs[:, b % 2, k * P:(k + 1) * P], identf[0:S, 0:S])
                t.then_inc(s("p_cT"), 1)

            def a_keys(b):
                pe.wait_ge(s("v_cL"), b + 1)
                for m in range(KC):
                    t = three(PJ[:, m * S:(m + 1) * S],
                              (lambda k: wH[:, 1, k, m * P:(m + 1) * P], lambda k: wL[:, 1, k, m * P:(m + 1) * P]),
                              (lambda k: cH[:, k, :], lambda k: cL[:, k, :]))
                t.then_inc(s("p_k"), 1)

            def a_values(b):
                t = three(TR[0:S, 0:D], (lambda k: cH[:, k, :], lambda k: cL[:, k, :]),
                          (lambda k: wH[:, 2, k, :], lambda k: wL[:, 2, k, :]))
                t.then_inc(s("p_v"), 1)

            def a_x_turn(b):
                pe.wait_ge(s("v_xn"), b + 1)
                turn4(lambda h, k: xn[:, h, k * P:(k + 1) * P]).then_inc(s("p_xT"), 1)

            def a_queries(b):
                pe.wait_ge(s("v_xL"), b + 1)
                for m in range(KC):
                    t = three(PJk[:, m, :],
                              (lambda k: wH[:, 0, k, m * P:(m + 1) * P], lambda k: wL[:, 0, k, m * P:(m + 1) * P]),
                              (lambda k: xH[:, k, :], lambda k: xL[:, k, :]))
                t.then_inc(s("p_q"), 1)

            def mx(b, i):
                h, c, q = i // 4, (i // 2) % 2, i % 2
                if i == 0:
                    pe.wait_ge(s("a_kb"), b + 1)
                    pe.wait_ge(s("v_tb"), b + 1)
                    pe.wait_ge(s("a_qH"), KC * (b + 1))
                n = NM * b + i
                if n >= 2:
                    pe.wait_ge(s("v_mx"), n - 1)
                o = MX[i % 2][:, 0:G * S]
                hd = c * HC + q * G
                pe.matmul(o, qH[:, b % 3, c, h * P:(h + 1) * P], kbH[:, b % 3, hd:hd + G, :], start=True, stop=False)
                pe.matmul(o, identb[:, :], tb[:, b % 2, h, c, 0:S].unsqueeze(1).to_broadcast([P, G, S]),
                          start=False, stop=True).then_inc(s("p_mx"), 1)

            def turn_bias(b):
                pe.wait_ge(s("v_mx"), NM * (b + 1))
                for c in range(KC):
                    for h in range(TH):
                        t = pe.transpose(RTb[:, c, h * P:(h + 1) * P], tb[:, b % 2, h, c, :], identb[:, :])
                t.then_inc(s("p_T"), 1)

            def st(b, f):
                n = NF * b + f
                if f == 0:
                    pe.wait_ge(s("a_T"), b + 1)
                    pe.wait_ge(s("v_kbL"), b + 1)
                    pe.wait_ge(s("v_qL"), b + 1)
                if n >= 2:
                    pe.wait_ge(s("a_exp"), n - 1)
                for j in range(2):
                    hd = 2 * f + j
                    c = hd // HC
                    o = ST[f % 2][0:S, j * T:(j + 1) * T]
                    pe.matmul(o, kbH[:, b % 3, hd, :], qH[:, b % 3, c, :], start=True, stop=False)
                    pe.matmul(o, kbL[:, b % 2, hd, :], qH[:, b % 3, c, :], start=False, stop=False)
                    pe.matmul(o, kbH[:, b % 3, hd, :], qL[:, b % 3, c, :], start=False, stop=False)
                    t = pe.matmul(o, sel[:, hd % HC, :], tT[:, b % 2, c, :], start=False, stop=True)
                t.then_inc(s("p_st"), 1)

            def pv(b, g):
                pe.wait_ge(s("a_exp"), NF * b + 2 * g + 2)
                pe.wait_ge(s("v_va"), b + 1)
                if g % 2 == 0 and (b or g):
                    pe.wait_ge(s("a_ov"), 2 * b + g // 2)
                for j in range(G):
                    hd = G * g + j
                    t = pe.matmul(OVg[32 * j:32 * j + 32, g % 2, :], va[:, b % 3, hd, :, :],
                                  pr[:, (hd // 2) % PR, hd % 2, :], start=True, stop=True)
                t.then_inc(s("p_pv"), 1)

            def c_out_turn(b):
                pe.wait_ge(s("a_ov"), 2 * b + 2)
                for h, bank in enumerate((TR, PJ)):
                    if h == 0:
                        read("v_va", b + 3)
                        read("v_hL", b - 1)
                    else:
                        read("v_kL", b + 3)
                    for g in range(H // G):
                        t = pe.transpose(bank[:, g * P:(g + 1) * P], ou[:, g, h * P:(h + 1) * P], identf[:, :])
                    t.then_inc(s("p_ot"), 1)

            def c_norm_turn(b):
                pe.wait_ge(s("v_on"), TH * (b + 1))
                turn4(lambda h, k: on[:, h, k * P:(k + 1) * P]).then_inc(s("p_on"), 1)

            def c_project(b):
                pe.wait_ge(s("v_onL"), b + 1)
                for h in range(TH):
                    t = three(PJk[:, h, :],
                              (lambda k: oH[:, k, h * P:(h + 1) * P], lambda k: oL[:, k, h * P:(h + 1) * P]),
                              (lambda k: wH[:, 3, k, :], lambda k: wL[:, 3, k, :]))
                t.then_inc(s("p_op"), 1)

            def c_hidden_turn(b):
                pe.wait_ge(s("v_hn"), b + 1)
                turn4(lambda h, k: hn[:, TH * b + h, k * P:(k + 1) * P]).then_inc(s("p_hT"), 1)

            def c_logits(b):
                pe.wait_ge(s("v_hL"), b + 1)
                hi, lo = hidden_buf(b)
                t = three(RT[0:E, 0:T], (lambda k: rH[:, k, :], lambda k: rL[:, k, :]),
                          (lambda k: hi[:, k, :], lambda k: lo[:, k, :]))
                t.then_inc(s("p_lg"), 1)

            def r_turn(b):
                pe.wait_ge(s("a_lg"), b + 1)
                for h in range(TH):
                    t = pe.transpose(RT[:, h * E:(h + 1) * E], lgT[:, h * P:(h + 1) * P], identf[0:E, 0:E])
                t.then_inc(s("p_lt"), 1)

            def r_gates_turn(b):
                pe.wait_ge(s("v_dsp"), b + 1)
                for h in range(TH):
                    t = pe.transpose(RT[0:E, h * P:(h + 1) * P], dsp[:, b % 2, h, :], identf[:, :])
                t.then_inc(s("p_dT"), 1)

            def r_bias(b):
                for h in range(TH):
                    t = pe.matmul(RTk[:, h, :], dT[:, h * P:(h + 1) * P], eb[:, :], start=True, stop=True)
                t.then_inc(s("p_bs"), 1)

            def r_ranks():
                n = NS * E
                pe.matmul(RT[:, 0:n], utri[:, :], oh[:, 0:NS, :], start=True, stop=False)
                pe.matmul(RT[:, 0:n], onesb[:, :], cum[:, 0:NS, :], start=False, stop=True)
                pe.matmul(RT[:, n:n + E], onesb[:, :], cum[:, NS, :], start=True, stop=True).then_inc(s("p_rk"), 1)

            experts = {}

            def block_step(j):
                if j < NB:
                    if j == 0:
                        pe.wait_ge(s("v_be"), 1)
                        pe.wait_ge(s("v_dn"), NU)
                    experts[j] = pe.value_load(be[0:1, j:j + 1], min_val=0, max_val=E - 1)
                    pe.wait_ge(s(f"d_hb{j % HR}"), 16 * (j // HR + 1))
                    if j >= 2:
                        pe.wait_ge(s("v_bL"), j - 1)
                    for k in range(KC):
                        t = pe.transpose(TURN[j % 2][:, k * P:(k + 1) * P], hb[:, j % HR, k * P:(k + 1) * P], identf[:, :])
                    t.then_inc(s("p_bT"), 1)
                if j >= 1:
                    m = j - 1
                    e = experts.pop(m)
                    pe.wait_ge(s("v_bL"), m + 1)
                    if m >= 2:
                        pe.wait_ge(s("a_y"), m - 1)
                    three(PROD[m % 2].rearrange("p (o d) -> p o d", o=1),
                          (lambda k: bH[:, m % 2, k, :], lambda k: bL[:, m % 2, k, :]),
                          (lambda k: eH[:, k, bass.ds(e, 1), :], lambda k: eL[:, k, bass.ds(e, 1), :])).then_inc(s("p_by"), 1)

            def dense_unit(u):
                b, p, h, bank = unit(u)
                if u == 0:
                    pe.wait_ge(s("v_e"), KC)
                if u % NU == 0:
                    pe.wait_ge(s("v_hL"), b + 1)
                if u == 0:
                    pe.wait_ge(s("a_exp"), NF * B)
                if u >= 4:
                    pe.wait_ge(s("v_dn"), u - 3)
                if u == NU:
                    pe.wait_ge(s("a_y"), NB)
                hi, lo = hidden_buf(b)
                three(bank[:, :].rearrange("p (e d) -> p e d", e=2),
                      (lambda k: hi[:, k, h * P:(h + 1) * P], lambda k: lo[:, k, h * P:(h + 1) * P]),
                      (lambda k: eH[:, k, 2 * p:2 * p + 2, :], lambda k: eL[:, k, 2 * p:2 * p + 2, :])).then_inc(s("p_dn"), 1)

            def read(name, b, per=1):
                if 0 <= b < B:
                    pe.wait_ge(s(name), per * (b + 1))

            a_ctx_turn(0)
            for i in ITER:
                A, M, C, R = i + 2, i + 1, i - 1, i - 2
                isA, isM, isS, isC, isR = (0 <= n < B for n in (A, M, i, C, R))
                for f in range(NF):
                    if isS and f:
                        st(i, f)
                    if isM:
                        for n in MAXIMA[f]:
                            mx(M, n)
                    if f == 0:
                        if isC:
                            pv(C, 3)
                        if isA:
                            read("v_x1", R)
                            read("v_qL", M)
                            if i == -2:
                                pe.wait_ge(s("v_w"), 4)
                            a_keys(A)
                        if isS:
                            st(i, f)
                    if f == 1:
                        if isA:
                            read("v_hL", R)
                            a_values(A)
                        if isR:
                            read("a_T", i)
                            read("v_acc", R - 1)
                            if R == 0:
                                pe.wait_ge(s("v_r"), 1)
                            c_logits(R)
                    if f == 2:
                        if isC:
                            c_out_turn(C)
                        if isR:
                            r_turn(R)
                    if f == 3:
                        if isS:
                            pv(i, 0)
                        if isA:
                            read("v_va", A)
                            if isC:
                                pe.wait_ge(s("v_on"), TH * C + 1)
                            a_x_turn(A)
                    if f == 4:
                        if isC:
                            read("v_xL", A)
                            c_norm_turn(C)
                        if isA:
                            read("v_kL", A)
                            a_queries(A)
                    if f == 5:
                        if isS:
                            pv(i, 1)
                        if isC:
                            read("v_qL", A)
                            c_project(C)
                        if isR:
                            r_gates_turn(R)
                    if f == 6:
                        if i + 3 < B:
                            read("v_onL", C)
                            read("v_xL", A)
                            a_ctx_turn(i + 3)
                        if isR:
                            pe.wait_ge(s("a_dT"), R + 1)
                            if R == SB - 1:
                                r_ranks()
                                pe.wait_ge(s("v_rk"), 1)
                            r_bias(R)
                    if f == 7:
                        if isC:
                            read("v_cL", i + 3)
                            c_hidden_turn(C)
                        if isM:
                            read("v_acc", R)
                            turn_bias(M)
                        if isS:
                            pv(i, 2)
                    for u in dense(i, f):
                        dense_unit(u)
                    for j in steps(i, f):
                        block_step(j)
            for j in STEPS_LEFT:
                block_step(j)
            for u in DENSE_LEFT:
                dense_unit(u)

        @block.scalar
        def _(act):
            for i in range(4):
                act.wait_ge(s("p_w"), i + 1)
                act.activation(wH[:, i, :, :], WB[i][:, :], ACT.Copy).then_inc(s("a_w"), 1)

            def block_part(j):
                if j < NB:
                    act.wait_ge(s("p_bT"), j + 1)
                    if j >= 2:
                        act.wait_ge(s("p_by"), j - 1)
                    act.activation(bH[:, j % 2, :, :], TURN[j % 2], ACT.Copy).then_inc(s("a_bH"), 1)
                if j >= 1:
                    m = j - 1
                    act.wait_ge(s("p_by"), m + 1)
                    if m >= HR:
                        act.wait_ge(s(f"d_ys{m % HR}"), 16 * (m // HR))
                    act.activation(yb[:, m % HR, :], PROD[m % 2], ACT.Copy).then_inc(s("a_y"), 1)

            def exp(b, f):
                n = NF * b + f
                act.wait_ge(s("p_st"), n + 1)
                if n >= PR:
                    act.wait_ge(s("p_pv"), (n - PR) // 2 + 1)
                act.activation(pr[:, f % PR, :, :], ST[f % 2][0:S, :], ACT.Exp, scale=SCALE).then_inc(s("a_exp"), 1)

            def out_copy(b, half):
                act.wait_ge(s("p_pv"), 4 * b + 2 * half + 2)
                if b >= 1:
                    act.wait_ge(s("p_ot"), TH * b)
                act.activation(ou[:, 2 * half:2 * half + 2, :], OVg, ACT.Copy).then_inc(s("a_ov"), 1)

            def ctx_high(b):
                act.wait_ge(s("p_cT"), b + 1)
                if b >= 1:
                    act.wait_ge(s("p_v"), b)
                act.activation(cH[:, :, :], TR[:, 0:KC * S], ACT.Copy).then_inc(s("a_cH"), 1)

            def keys_high(b):
                act.wait_ge(s("p_k"), b + 1)
                if b >= 1:
                    act.wait_ge(s("v_kL"), b)
                    act.wait_ge(s("a_kb"), b)
                for m in range(KC):
                    act.activation(kH[:, m, :], PJ[:, m * S:(m + 1) * S], ACT.Identity,
                                   bias=bk_c[:, m:m + 1]).then_inc(s("a_kH"), 1)

            def keys_masked(b, n0, n1):
                if n0 == 0:
                    act.wait_ge(s("a_kH"), KC * (b + 1))
                    if b >= 3:
                        act.wait_ge(s("p_st"), NF * (b - 2))
                for h in range(n0, n1):
                    a = act.activation(kbH[:, b % 3, h, :], kH[:, h // HC, :].bitcast(F32), ACT.Copy,
                                       scale=ind[:, h % HC:h % HC + 1])
                if n1 == H:
                    a.then_inc(s("a_kb"), 1)

            def x_high(b):
                act.wait_ge(s("p_xT"), b + 1)
                if b >= 1:
                    act.wait_ge(s("p_q"), b)
                act.activation(xH[:, :, :], TR[:, :], ACT.Copy).then_inc(s("a_xH"), 1)

            def queries_high(b):
                act.wait_ge(s("p_q"), b + 1)
                for m in range(KC):
                    act.activation(qH[:, b % 3, m, :], PJk[:, m, :], ACT.Identity,
                                   bias=bq_c[:, m:m + 1]).then_inc(s("a_qH"), 1)

            def gate_exp(b):
                act.wait_ge(s("v_lc"), b + 1)
                act.activation(le[:, :, :], lc[:, :, :], ACT.Exp).then_inc(s("a_le"), 1)

            def norm_high(b):
                act.wait_ge(s("p_on"), b + 1)
                if b >= 1:
                    act.wait_ge(s("p_op"), b)
                act.activation(oH[:, :, :], TR[:, :], ACT.Copy).then_inc(s("a_onH"), 1)

            def hidden_high(b):
                act.wait_ge(s("p_hT"), b + 1)
                if b >= 1:
                    act.wait_ge(s("p_lg"), b)
                act.activation(hidden_buf(b)[0][:, :, :], TR[:, :], ACT.Copy).then_inc(s("a_hH"), 1)

            def bias_copy(b):
                act.wait_ge(s("p_T"), b + 1)
                if b >= 2:
                    act.wait_ge(s("p_st"), NF * (b - 1))
                act.activation(tT[:, b % 2, :, :], RTb, ACT.Copy).then_inc(s("a_T"), 1)

            def gates_copy(b):
                act.wait_ge(s("p_dT"), b + 1)
                act.activation(dT[:, :], RT[0:E, 0:T], ACT.Copy).then_inc(s("a_dT"), 1)

            def logits_copy(b):
                act.wait_ge(s("p_lg"), b + 1)
                act.activation(lgT[:, :], RT[0:E, 0:T], ACT.Copy).then_inc(s("a_lg"), 1)

            act.wait_ge(s("d_bias"), 16 * 8)
            act.wait_ge(s("c_pool"), 19)
            ctx_high(0)
            MASKED = [0, 0, 3, 6, 9, 12, 15, H, H]
            for i in ITER:
                A, M, C, R = i + 2, i + 1, i - 1, i - 2
                isA, isM, isS, isC, isR = (0 <= n < B for n in (A, M, i, C, R))
                for f in range(NF):
                    if f == 0:
                        if isC:
                            out_copy(C, 1)
                        if isA:
                            keys_high(A)
                    if isS:
                        exp(i, f)
                    if f == 1 and isR:
                        logits_copy(R)
                    if f == 3:
                        if isR:
                            gate_exp(R)
                        if isA:
                            x_high(A)
                    if f == 4:
                        if isC:
                            norm_high(C)
                        if isA:
                            queries_high(A)
                    if f == 5:
                        if isS:
                            out_copy(i, 0)
                        if isR:
                            gates_copy(R)
                    if f == 6 and i + 3 < B:
                        ctx_high(i + 3)
                    if f == 7:
                        if isC:
                            hidden_high(C)
                        if isM:
                            bias_copy(M)
                    if isA and MASKED[f + 1] > MASKED[f]:
                        keys_masked(A, MASKED[f], MASKED[f + 1])
                    for j in steps(i, f):
                        block_part(j)
                if i == -1:
                    act.activation(rH[:, :, :], r_nat[:, :, :], ACT.Copy).then_inc(s("a_r"), 1)
                if i in (0, 2):
                    k = i // 2
                    act.wait_ge(s("d_e"), 16 * (k + 1))
                    act.activation(eH[:, k, :, :], e_nat[:, :, :], ACT.Copy).then_inc(s("a_e"), 1)
            for j in STEPS_LEFT:
                block_part(j)

        @block.vector
        def _(v):
            cnt = [0]

            def link(ins):
                cnt[0] += 1
                ins.then_inc(s("dve"), 1)
                v.wait_ge(s("dve"), cnt[0])

            v.memset(zer[:, :], 0.0).then_inc(s("c_dve"), 1)
            v.memset(va[:, :, :, 1, :], 1.0).then_inc(s("c_dve"), 1)
            v.memset(cum[:, :, :], 0.0).then_inc(s("c_dve"), 1)
            v.wait_ge(s("c_pool"), 19)

            def ln_stats(src, stt, mvt, vet, name):
                for h in range(TH):
                    i = v.bn_stats(stt[:, h, :], src(h))
                link(i)
                for h in range(TH):
                    i = v.bn_aggr(mvt[:, h, :], stt[:, h, :])
                link(i)
                v.tensor_scalar(vet[:, :], mvt[:, :, 1], EPS, None, ALU.add).then_inc(s(name), 1)

            def ln1_stats(b):
                v.wait_ge(s(f"d_x{b}"), 16)
                if b >= 1:
                    v.wait_ge(s("g_r1"), b)
                ln_stats(lambda h: xr[:, b, h, :], st1, mv1, ve1, "v_ve1")

            def ln1_apply(b):
                v.wait_ge(s("g_r1"), b + 1)
                if b >= 1:
                    v.wait_ge(s("p_xT"), b)
                for h in range(TH):
                    i = v.tensor_scalar(xn[:, h, :], xr[:, b, h, :], mv1[:, h, 0:1], rs1[:, h:h + 1],
                                        ALU.subtract, ALU.mult)
                i.then_inc(s("v_xn"), 1)

            def ctx_low(bn):
                v.wait_ge(s("a_cH"), bn + 1)
                v.tensor_tensor(cL[:, :, :], TR[:, 0:KC * S].rearrange("p (k s) -> p k s", k=KC),
                                cH[:, :, :].bitcast(F32), ALU.subtract).then_inc(s("v_cL"), 1)

            def keys_values(bn):
                pn = bn % 3
                v.wait_ge(s("a_kH"), KC * (bn + 1))
                for m in range(KC):
                    i = v.scalar_tensor_tensor(out=kL[:, bn % 2, m, :], in0=PJ[:, m * S:(m + 1) * S],
                                               scalar=bk_c[:, m:m + 1], in1=kH[:, m, :].bitcast(F32),
                                               op0=ALU.add, op1=ALU.subtract)
                i.then_inc(s("v_kL"), 1)
                v.wait_ge(s("p_v"), bn + 1)
                if bn >= 3:
                    v.wait_ge(s("p_pv"), 4 * (bn - 2))
                v.tensor_tensor(va[:, pn, :, 0, :], TR[0:S, 0:D].rearrange("p (h d) -> p h d", h=H),
                                bv_b[0:S, :].rearrange("p (h d) -> p h d", h=H), ALU.add).then_inc(s("v_va"), 1)

            def keys_low(bn):
                v.wait_ge(s("v_kL"), bn + 1)
                if bn >= 2:
                    v.wait_ge(s("p_st"), NF * (bn - 1))
                for m in range(KC):
                    i = v.tensor_tensor(kbL[:, bn % 2, m * HC:(m + 1) * HC, :],
                                        kL[:, bn % 2, m, :].unsqueeze(1).to_broadcast([P, HC, S]),
                                        ind[:, :].unsqueeze(2).to_broadcast([P, HC, S]), ALU.mult)
                i.then_inc(s("v_kbL"), 1)

            def mask_bias(bn):
                pn = bn % 2
                v.wait_ge(s(f"d_k{pn}"), 16 * (bn // 2 + 1))
                if bn >= 2:
                    v.wait_ge(s("p_T"), bn - 1)
                for c in range(KC):
                    i = v.scalar_tensor_tensor(out=tb[:, pn, :, c, 0:S],
                                               in0=kp8[:, pn, :].unsqueeze(1).to_broadcast([P, TH, S]),
                                               scalar=-BIG, in1=attnb[:, :, :], op0=ALU.mult, op1=ALU.add)
                i.then_inc(s("v_tb"), 1)
                v.wait_ge(s("v_tb"), bn + 1)
                link(v.tensor_reduce(mb[:, :], tb[:, pn, :, 0, 0:S], AX_X, ALU.max))
                link(v.tensor_scalar(mg[:, :], mb[:, :], -1.0, None, ALU.is_ge))
                link(v.reciprocal(mr[:, :], mg[:, :]))
                link(v.tensor_tensor(nanf[:, bn % 4, :], mg[:, :], mr[:, :], ALU.mult))

            def x_low(bn):
                v.wait_ge(s("a_xH"), bn + 1)
                v.tensor_tensor(xL[:, :, :], TRk, xH[:, :, :].bitcast(F32), ALU.subtract).then_inc(s("v_xL"), 1)

            def queries_low(bn):
                pn = bn % 3
                v.wait_ge(s("a_qH"), KC * (bn + 1))
                if bn >= 3:
                    v.wait_ge(s("p_st"), NF * (bn - 2))
                for m in range(KC):
                    i = v.scalar_tensor_tensor(out=qL[:, pn, m, :], in0=PJk[:, m, :], scalar=bq_c[:, m:m + 1],
                                               in1=qH[:, pn, m, :].bitcast(F32), op0=ALU.add, op1=ALU.subtract)
                i.then_inc(s("v_qL"), 1)

            def route_logits(b):
                v.wait_ge(s("p_lt"), b + 1)
                link(v.tensor_tensor(lg[:, :, :], RT[:, 0:TH * E].rearrange("p (h e) -> p h e", h=TH),
                                     rb_b[:, :].unsqueeze(1).to_broadcast([P, TH, E]), ALU.add))
                for h in range(TH):
                    i = v.max(mx8[:, h, :], lg[:, h, :])
                link(i)
                v.tensor_tensor(lc[:, :, :], lg[:, :, :], mx8[:, :, 0:1].to_broadcast([P, TH, E]),
                                ALU.subtract).then_inc(s("v_lc"), 1)
                for h in range(TH):
                    i = v.max_index(ix8[:, h, :], mx8[:, h, :], lg[:, h, :])
                link(i)
                link(v.tensor_copy(ixf[:, :], ix8[:, :, 0]))

            def route_choice(b):
                for h in range(TH):
                    i = v.tensor_scalar(oh[:, TH * b + h, :], iota8[:, :], ixf[:, h:h + 1], None, ALU.is_equal)
                link(i)
                if b < SB:
                    for h in range(TH):
                        t = TH * b + h
                        link(v.tensor_tensor(cum[:, t + 1, :], cum[:, t, :], oh[:, t, :], ALU.add))
                v.wait_ge(s("a_le"), b + 1)
                link(v.tensor_reduce(sm[:, :], le[:, :, :], AX_X, ALU.add))
                link(v.reciprocal(gts[:, TH * b:TH * b + TH], sm[:, :]))
                for h in range(TH):
                    i = v.tensor_scalar(dsp[:, b % 2, h, :], oh[:, TH * b + h, :], gts[:, TH * b + h:TH * b + h + 1], None, ALU.mult)
                i.then_inc(s("v_dsp"), 1)

            def add_bias(b):
                v.wait_ge(s("p_bs"), b + 1)
                v.tensor_tensor(xr[:, b, :, :], xr[:, b, :, :], RTk, ALU.add).then_inc(s("v_acc"), 1)

            def ranks_copy():
                v.wait_ge(s("p_rk"), 1)
                v.tensor_copy(tot[:, :], RT[:, NS * E:NS * E + E])
                v.tensor_copy(rk[:, :, :], RT[:, 0:NS * E].rearrange("p (t e) -> p t e", t=NS)).then_inc(s("v_rk"), 1)

            def places():
                v.wait_ge(s("v_rk"), 1)
                link(v.tensor_tensor(cmpn[:, :, :], tot[:, :].unsqueeze(2).to_broadcast([P, E, NS]),
                                     j128[:, :].unsqueeze(1).to_broadcast([P, E, NS]), ALU.is_gt))
                link(v.tensor_reduce(nblk[:, :], cmpn[:, :, :], AX_X, ALU.add))
                link(v.tensor_tensor(trin[:, :, :], tri8[:, :, :], nblk[:, :].unsqueeze(1).to_broadcast([P, E, E]), ALU.mult))
                link(v.tensor_reduce(sbk[:, :], trin[:, :, :], AX_X, ALU.add))
                v.tensor_scalar(base[:, :], sbk[:, :], float(P), None, ALU.mult)
                link(v.tensor_tensor(endb[:, :], sbk[:, :], nblk[:, :], ALU.add))
                link(v.tensor_tensor(rk2[:, :, :], rk[:, :, :], base[:, :].unsqueeze(1).to_broadcast([P, NS, E]), ALU.add))
                link(v.tensor_tensor(rk[:, :, :], rk2[:, :, :], oh[:, 0:NS, :], ALU.mult))
                link(v.tensor_reduce(slotf[:, :], rk[:, :, :], AX_X, ALU.add))
                v.tensor_copy(slot[:, :], slotf[:, :]).then_inc(s("v_idx"), 1)
                link(v.tensor_tensor(cmpb[:, :, :], endb[:, :].unsqueeze(1).to_broadcast([P, NB, E]),
                                     jblk[:, :].unsqueeze(2).to_broadcast([P, NB, E]), ALU.is_le))
                link(v.tensor_reduce(bef[:, :], cmpb[:, :, :], AX_X, ALU.add))
                v.tensor_scalar(be[:, :], bef[:, :], float(E - 1), None, ALU.min).then_inc(s("v_be"), 1)

            def maxima(b, i):
                h, c, q = i // 4, (i // 2) % 2, i % 2
                v.wait_ge(s("p_mx"), NM * b + i + 1)
                v.tensor_reduce(tb[:, b % 2, h, c, S + q * G:S + (q + 1) * G],
                                MX[i % 2][:, 0:G * S].rearrange("p (g s) -> p g s", g=G),
                                AX_X, ALU.max, negate=True).then_inc(s("v_mx"), 1)

            def normalise(b):
                if b >= 1:
                    v.wait_ge(s("p_on"), b)
                for h, bank in enumerate((TR, PJ)):
                    v.wait_ge(s("p_ot"), TH * b + h + 1)
                    o4 = bank[:, :].rearrange("p (n z d) -> p n z d", n=H, z=2)
                    link(v.reciprocal(rd[:, h, :], o4[:, :, 1, 0]))
                    link(v.tensor_scalar(rdn[:, h, :], rd[:, h, :], nanf[:, b % 4, h:h + 1], None, ALU.mult))
                    v.tensor_tensor(on[:, h, :].rearrange("p (n d) -> p n d", n=H), o4[:, :, 0, :],
                                    rdn[:, h, :].unsqueeze(2).to_broadcast([P, H, DK]),
                                    ALU.mult).then_inc(s("v_on"), 1)

            def norm_low(b):
                v.wait_ge(s("a_onH"), b + 1)
                v.tensor_tensor(oL[:, :, :], TRk, oH[:, :, :].bitcast(F32), ALU.subtract).then_inc(s("v_onL"), 1)

            def residual(b):
                v.wait_ge(s("p_op"), b + 1)
                v.wait_ge(s("g_xbo"), b + 1)
                v.tensor_tensor(xr[:, b, :, :], xr[:, b, :, :], PJk, ALU.add).then_inc(s("v_x1"), 1)
                v.wait_ge(s("v_x1"), b + 1)
                if b >= 1:
                    v.wait_ge(s("g_r2"), b)
                ln_stats(lambda h: xr[:, b, h, :], st2, mv2, ve2, "v_ve2")

            def hidden(b):
                v.wait_ge(s("g_r2"), b + 1)
                for h in range(TH):
                    ins = v.tensor_scalar(hn[:, TH * b + h, :], xr[:, b, h, :], mv2[:, h, 0:1], rs2[:, h:h + 1],
                                          ALU.subtract, ALU.mult)
                ins.then_inc(s("v_hn"), 1)

            def hidden_low(b):
                v.wait_ge(s("a_hH"), b + 1)
                hi, lo = hidden_buf(b)
                v.tensor_tensor(lo[:, :, :], TRk, hi[:, :, :].bitcast(F32), ALU.subtract).then_inc(s("v_hL"), 1)

            def block_part(j):
                if j < NB:
                    v.wait_ge(s("a_bH"), j + 1)
                    v.tensor_tensor(bL[:, j % 2, :, :], TURN[j % 2].rearrange("p (k t) -> p k t", k=KC),
                                    bH[:, j % 2, :, :].bitcast(F32), ALU.subtract).then_inc(s("v_bL"), 1)

            def dense_part(u):
                b, p, h, bank = unit(u)
                v.wait_ge(s("v_dsp"), b + 1)
                v.wait_ge(s("p_dn"), u + 1)
                for e in range(2):
                    i = v.scalar_tensor_tensor(out=xr[:, b, h, :], in0=bank[:, e * D:(e + 1) * D],
                                               scalar=dsp[:, b % 2, h, 2 * p + e:2 * p + e + 1],
                                               in1=xr[:, b, h, :], op0=ALU.mult, op1=ALU.add)
                    if e == 0:
                        link(i)
                i.then_inc(s("v_dn"), 1)
                v.wait_ge(s("v_dn"), u + 1)

            def finish(t):
                v.wait_ge(s(f"d_gy{t}"), 16)
                b, h = t // TH, t % TH
                v.scalar_tensor_tensor(out=xr[:, b, h, :], in0=gy[:, t, :], scalar=gts[:, t:t + 1],
                                       in1=xr[:, b, h, :], op0=ALU.mult, op1=ALU.add).then_inc(s("v_fin"), 1)

            ln1_stats(0)
            for i in range(4):
                v.wait_ge(s("a_w"), i + 1)
                v.tensor_tensor(wL[:, i, :, :], WB[i][:, :].rearrange("p (k d) -> p k d", k=KC),
                                wH[:, i, :, :].bitcast(F32), ALU.subtract).then_inc(s("v_w"), 1)
                if i == 0:
                    ln1_apply(0)
            v.wait_ge(s("d_bias"), 16 * 8)
            link(v.tensor_scalar(attnb[:, :, :], am8[:, :, :], -BIG, None, ALU.mult))
            ctx_low(0)
            for i in ITER:
                A, M, C, R = i + 2, i + 1, i - 1, i - 2
                isA, isM, isS, isC, isR = (0 <= n < B for n in (A, M, i, C, R))
                for f in range(NF):
                    if f == 0 and isR:
                        hidden_low(R)
                    if f == 4 and isA:
                        x_low(A)
                    if f == 5 and isC:
                        norm_low(C)
                    if isM:
                        for n in MAXIMA[f]:
                            maxima(M, n)
                    if f == 0 and isM:
                        keys_low(M)
                    if f == 1 and isA:
                        keys_values(A)
                        if A:
                            ln1_stats(A)
                    if f == 2:
                        if A and isA:
                            ln1_apply(A)
                        if isC:
                            normalise(C)
                    if f == 3 and isR:
                        route_logits(R)
                    if f == 4 and isR:
                        route_choice(R)
                    if f == 5 and isA:
                        queries_low(A)
                        mask_bias(A)
                    if f == 6:
                        if isC:
                            residual(C)
                        if R == SB - 1:
                            ranks_copy()
                    if f == 7:
                        if isR:
                            add_bias(R)
                            v.wait_ge(s("v_acc"), R + 1)
                        if isC:
                            hidden(C)
                        if i + 3 < B:
                            ctx_low(i + 3)
                        if R == SB - 1:
                            places()
                    for u in dense_sum(i, f):
                        dense_part(u)
                    for j in steps(i, f):
                        block_part(j)
                if i == -1:
                    v.wait_ge(s("a_r"), 1)
                    v.tensor_tensor(rL[:, :, :], r_nat[:, :, :], rH[:, :, :].bitcast(F32), ALU.subtract).then_inc(s("v_r"), 1)
                if i in (0, 2):
                    k = i // 2
                    v.wait_ge(s("a_e"), k + 1)
                    v.tensor_tensor(eL[:, k, :, :], e_nat[:, :, :], eH[:, k, :, :].bitcast(F32),
                                    ALU.subtract).then_inc(s("v_e"), 1)
            for j in STEPS_LEFT:
                block_part(j)
            for u in DENSE_LEFT:
                dense_part(u)
            for t in range(NS):
                finish(t)


_INS = ['x', 'ctx_1024', 'mask_SxS2_bk1', 'mask_BxS2_bf0', 'L0_xattn_Wq', 'L0_xattn_bq', 'L0_xattn_Wk',
        'L0_xattn_bk', 'L0_xattn_Wv', 'L0_xattn_bv', 'L0_xattn_Wo', 'L0_xattn_bo', 'L0_ffn_router_w',
        'L0_ffn_router_b', 'L0_ffn_expert_w', 'L0_ffn_expert_b']
_OUTS = [((8, 256, 256), 'float32')]


def kernel(**inputs):
    import numpy as _np
    import concourse.bacc as _bacc
    from concourse import mybir as _mybir
    from concourse.bass_utils import run_bass_kernel_spmd as _run

    nc = _bacc.Bacc("TRN2", target_bir_lowering=False, num_devices=1)
    arrays, args = {}, []
    for name in _INS:
        a = _np.ascontiguousarray(inputs[name])
        arrays[f"in_{name}_dram"] = a
        args.append(nc.dram_tensor(f"in_{name}_dram", a.shape, _mybir.dt.from_np(a.dtype), kind="ExternalInput").ap())
    for i, (shape, dtype) in enumerate(_OUTS):
        dt = _mybir.dt.from_np(_np.dtype(dtype))
        args.append(nc.dram_tensor(f"out_{i}_dram", shape, dt, kind="ExternalOutput").ap())
    xattn_moe_kernel(nc, *args)
    r = _run(nc, [arrays], core_ids=[0])
    return r.results[0]["out_0_dram"]
```

```python
from contextlib import ExitStack

import concourse.bass as bass
from concourse import mybir

F32 = mybir.dt.float32
F32R = mybir.dt.float32r
BF16 = mybir.dt.bfloat16
U8 = mybir.dt.uint8
U32 = mybir.dt.uint32
ALU = mybir.AluOpType
ACT = mybir.ActivationFunctionType
AX_X = mybir.AxisListType.X

P = 128
BIG = float(2 ** 100)
EPS = 1e-5


def xattn_moe_kernel(nc, x, ctx_in, attn_mask, key_mask, Wq, bq, Wk, bk, Wv, bv, Wo, bo,
                     router_w, router_b, expert_w, expert_b, out):
    B, T, D = x.shape
    S = ctx_in.shape[1]
    E = router_w.shape[1]
    H = 16
    DK = D // H
    SCALE = 1.0 / float(DK) ** 0.5
    KC = D // P
    TH = T // P
    HC = H // KC
    G = 4
    NF = H // 2
    NM = TH * H // G
    NT = B * TH
    SB = B - 2
    NS = SB * TH
    NB = NS + E - 1
    EP = E // 2
    NU = TH * EP
    HR = 8

    es = ExitStack()
    scr_h = nc.dram_tensor("sorted_h", [NB * P, D], F32).ap()
    scr_y = nc.dram_tensor("sorted_y", [NB * P, D], F32).ap()
    with es:
        def sb(name, shape, dt=F32):
            return es.enter_context(nc.sbuf_tensor(name, shape, dt))

        def sem(name):
            return es.enter_context(nc.semaphore(name))

        identf = sb("identf", [P, P])
        identb = sb("identb", [P, P], BF16)
        sel = sb("sel", [P, HC, S], BF16)
        ind = sb("ind", [P, HC])
        iota8 = sb("iota8", [P, E])
        mhalf = sb("mhalf", [P, TH])
        w_nat = sb("w_nat", [P, 4, KC, D])
        wH = sb("wH", [P, 4, KC, D], F32R)
        wL = sb("wL", [P, 4, KC, D], F32R)
        e_nat = sb("e_nat", [P, E, D])
        eH = sb("eH", [P, KC, E, D], F32R)
        eL = sb("eL", [P, KC, E, D], F32R)
        r_nat = sb("r_nat", [P, KC, E])
        rH = sb("rH", [P, KC, E], F32R)
        rL = sb("rL", [P, KC, E], F32R)
        bq_c = sb("bq_c", [P, KC])
        bk_c = sb("bk_c", [P, KC])
        bv_b = sb("bv_b", [P, D])
        bo_b = sb("bo_b", [P, D])
        rb_b = sb("rb_b", [P, E])
        eb = sb("eb", [E, D])
        am8 = sb("am8", [P, TH, S], U8)
        attnb = sb("attnb", [P, TH, S])
        xr = sb("xr", [P, B, TH, D])
        ctxs = sb("ctxs", [S, 2, D])
        kp8 = sb("kp8", [P, 2, S], U8)
        st1 = sb("st1", [P, TH, 6])
        mv1 = sb("mv1", [P, TH, 2])
        rs1 = sb("rs1", [P, TH])
        ve1 = sb("ve1", [P, TH])
        xn = sb("xn", [P, TH, D])
        xH = sb("xH", [P, KC, T], F32R)
        xL = sb("xL", [P, KC, T], F32R)
        qH = sb("qH", [P, 3, KC, T], F32R)
        qL = sb("qL", [P, 3, KC, T], F32R)
        cH = sb("cH", [P, KC, S], F32R)
        cL = sb("cL", [P, KC, S], F32R)
        kH = sb("kH", [P, KC, S], F32R)
        kL = sb("kL", [P, 2, KC, S])
        kbH = sb("kbH", [P, 3, H, S], F32R)
        kbL = sb("kbL", [P, 2, H, S], F32R)
        va = sb("va", [S, 3, H, 2, DK])
        tb = sb("tb", [P, 2, TH, KC, P], BF16)
        tT = sb("tT", [P, 2, KC, T], BF16)
        mg = sb("mg", [P, TH])
        mr = sb("mr", [P, TH])
        nanf = sb("nanf", [P, 2, TH])
        PR = 4
        assert PR * 2 * T == 4 * KC * D
        pr = w_nat[0:S, :, :, :].rearrange("p w k d -> p (w k d)").rearrange(
            "p (r j t) -> p r j t", r=PR, j=2)
        ou = sb("ou", [P, H // G, T])
        rd = sb("rd", [P, TH, H])
        rdn = sb("rdn", [P, TH, H])
        on = sb("on", [P, TH, D])
        oH = sb("oH", [P, KC, T], F32R)
        oL = sb("oL", [P, KC, T], F32R)
        st2 = sb("st2", [P, TH, 6])
        mv2 = sb("mv2", [P, TH, 2])
        rs2 = sb("rs2", [P, TH])
        ve2 = sb("ve2", [P, TH])
        hn = sb("hn", [P, NT, D])
        hH = sb("hH", [P, KC, T], F32R)
        hL = sb("hL", [P, KC, T], F32R)
        utri = sb("utri", [P, P], BF16)
        onesb = sb("onesb", [P, P], BF16)
        tri8 = sb("tri8", [P, E, E])
        j128 = sb("j128", [P, NS])
        jblk = sb("jblk", [P, NB])
        zer = sb("zer", [P, D])
        oh = sb("oh", [P, NT, E], BF16)
        cum = sb("cum", [P, NS + 1, E], BF16)
        gts = sb("gts", [P, NT])
        tot = sb("tot", [P, E])
        cmpn = sb("cmpn", [P, E, NS])
        nblk = sb("nblk", [P, E])
        trin = sb("trin", [P, E, E])
        sbk = sb("sbk", [P, E])
        endb = sb("endb", [P, E])
        base = sb("base", [P, E])
        rk = sb("rk", [P, NS, E])
        rk2 = sb("rk2", [P, NS, E])
        slotf = sb("slotf", [P, NS])
        slot = sb("slot", [P, NS], U32)
        cmpb = sb("cmpb", [P, NB, E])
        bef = sb("bef", [P, NB])
        be = sb("be", [P, NB], mybir.dt.int32)
        hb = e_nat[:, 0:HR, :]
        yb = w_nat[:, :, :, :].rearrange("p w k d -> p (w k) d")[:, 0:HR, :]
        bH = sb("bH", [P, 3, KC, P], F32R)
        bL = sb("bL", [P, 3, KC, P], F32R)
        gy = hn
        lgT = sb("lgT", [E, T])
        lg = sb("lg", [P, TH, E])
        mx8 = sb("mx8", [P, TH, 8])
        ix8 = sb("ix8", [P, TH, 8], U32)
        ixf = sb("ixf", [P, TH])
        lc = sb("lc", [P, TH, E])
        le = sb("le", [P, TH, E])
        sm = sb("sm", [P, TH])
        dsp = sb("dsp", [P, 2, TH, E])
        dT = sb("dT", [E, T])

        ps = [es.enter_context(nc.psum_tensor(f"ps{i}", [P, 512], F32)) for i in range(8)]
        TR, PJ, OV = ps[0], ps[1], ps[7]
        MX = [ps[2], ps[3]]
        ST = [ps[4], ps[5]]
        RT = ps[6]
        RTk = RT[:, :].rearrange("p (k t) -> p k t", k=KC)
        TRk = TR[:, :].rearrange("p (k t) -> p k t", k=KC)
        PJk = PJ[:, :].rearrange("p (k t) -> p k t", k=KC)
        OVg = OV[:, :].rearrange("p (g t) -> p g t", g=2)

        ORDER = (1, 2, 0, 3)
        WB = [MX[0], MX[1], ST[0], ST[1]]

        S_ = {}

        def s(name):
            if name not in S_:
                S_[name] = sem(name)
            return S_[name]

        for n in ("d_w0 d_w1 d_w2 d_w3 d_e d_bias d_z d_c0 d_c1 d_k0 d_k1 d_out d_sc "
                  "c_pool c_dve p_w p_dn v_dn a_T a_tb a_dT a_w v_w g_eH g_e "
                  "g_r1 g_r2 p_xT p_q p_cT p_k p_v p_st p_pv p_mx p_T p_ot p_on p_op p_hT p_lg p_lt p_dT p_bs "
                  "a_xH a_qH a_cH a_kH a_kb a_exp a_onH a_hH a_lg a_le "
                  "v_ve1 v_xn v_xL v_qL v_cL v_kL v_kbL v_va v_tb v_mx v_on v_onL v_x1 v_ve2 v_hn v_hL v_lc v_dsp v_acc "
                  "a_ov g_xbo v_rk a_r v_r p_rk v_be v_idx p_bT a_bH v_bL p_by a_y v_fin "
                  "dve").split() + [f"d_x{b}" for b in range(B)] + [f"d_hb{i}" for i in range(HR)] + [f"d_gy{i}" for i in range(NS)] + [f"d_ys{i}" for i in range(HR)]:
            s(n)

        block = es.enter_context(nc.Block())

        ITER = range(-2, B + 2)
        MAXIMA = [[0, 1], [2], [3], [4], [5], [6], [7], []]
        FIRST_MAXIMA = [[0, 1], [2, 3], [4], [5], [6], [7], [], []]

        def hidden_buf(b):
            return (xH, xL) if b == B - 1 else (hH, hL)

        UB = [OV, ST[0], ST[1]] + [OV] * (NU - 3) + [(OV, PJ, TR)[n % 3] for n in range(NU)]

        def unit(u):
            b, n = SB + u // NU, u % NU
            return b, n // TH, n % TH, UB[u]

        TURN = [MX[0][:, 0:D], MX[1][:, 0:D]]
        PROD = [ST[0][:, 0:D], ST[1][:, 0:D]]

        @block.sync
        def _(sp):
            def load(b):
                sp.dma_start(xr[:, b, :, :], x[b].rearrange("(h p) d -> p h d", p=P)).then_inc(s(f"d_x{b}"), 16)
                if b >= 2:
                    sp.wait_ge(s("p_cT"), b - 1)
                sp.dma_start(ctxs[:, b % 2, :], ctx_in[b]).then_inc(s(f"d_c{b % 2}"), 16)
                if b >= 2:
                    sp.wait_ge(s("v_tb"), b - 1)
                sp.dma_start(kp8[:, b % 2, :], key_mask[b].partition_broadcast(P)).then_inc(s(f"d_k{b % 2}"), 16)

            load(0)
            for i, w in ((1, Wk), (2, Wv), (0, Wq), (3, Wo)):
                sp.dma_start(w_nat[:, i, :, :], w.rearrange("(k p) d -> p k d", p=P)).then_inc(s(f"d_w{i}"), 16)
            sp.dma_start(bq_c[:, :], bq.rearrange("(m p) -> p m", p=P), allow_slow_non_contiguous=True).then_inc(s("d_bias"), 16)
            sp.dma_start(bk_c[:, :], bk.rearrange("(m p) -> p m", p=P), allow_slow_non_contiguous=True).then_inc(s("d_bias"), 16)
            sp.dma_start(am8[:, :, :], attn_mask.rearrange("(h p) s -> p h s", p=P)).then_inc(s("d_bias"), 16)
            sp.dma_start(bo_b[:, :], bo.partition_broadcast(P)).then_inc(s("d_bias"), 16)
            sp.dma_start(bv_b[:, :], bv.partition_broadcast(P)).then_inc(s("d_bias"), 16)
            sp.dma_start(rb_b[:, :], router_b.partition_broadcast(P)).then_inc(s("d_bias"), 16)
            sp.dma_start(eb[:, :], expert_b).then_inc(s("d_bias"), 16)
            sp.dma_start(r_nat[:, :, :], router_w.rearrange("(k p) e -> p k e", p=P)).then_inc(s("d_bias"), 16)
            load(1)
            sp.dma_start(e_nat[:, :, :], expert_w.rearrange("e (k p) d -> k p e d", p=P)[0]).then_inc(s("d_e"), 16)
            sp.wait_ge(s("c_dve"), 3)
            sp.dma_start(scr_h.rearrange("(p n) d -> p n d", p=P),
                         zer[:, :].unsqueeze(1).to_broadcast([P, NB, D])).then_inc(s("d_z"), 16)
            load(2)
            load(3)
            sp.wait_ge(s("g_e"), EP)
            sp.dma_start(e_nat[:, :, :], expert_w.rearrange("e (k p) d -> k p e d", p=P)[1]).then_inc(s("d_e"), 16)
            for b in range(4, B):
                load(b)

            def load_block(j):
                if j >= HR:
                    sp.wait_ge(s("p_bT"), j - HR + 1)
                sp.dma_start(hb[:, j % HR, :], scr_h[j * P:(j + 1) * P, :]).then_inc(s(f"d_hb{j % HR}"), 16)

            def store_block(j):
                sp.wait_ge(s("a_y"), j + 1)
                sp.dma_start(scr_y[j * P:(j + 1) * P, :], yb[:, j % HR, :]).then_inc(s(f"d_ys{j % HR}"), 16)

            sp.wait_ge(s("g_e"), KC * EP)
            sp.wait_ge(s("d_sc"), 16 * NS)
            for j in range(HR):
                load_block(j)
            for j in range(NB):
                if j + HR < NB:
                    load_block(j + HR)
                store_block(j)
            for t in list(range(NS, NT)) + list(range(NS)):
                if t < NS:
                    sp.wait_ge(s("v_fin"), t + 1)
                else:
                    sp.wait_ge(s("v_dn"), (t // TH - SB) * NU + (EP - 1) * TH + t % TH + 1)
                sp.dma_start(out[t // TH, (t % TH) * P:(t % TH + 1) * P, :], xr[:, t // TH, t % TH, :]).then_inc(s("d_out"), 16)
            sp.wait_ge(s("d_out"), 16 * NT)

        @block.gpsimd
        def _(pool):
            c = s("c_pool")
            pool.memset(identf[:, :], 0.0).then_inc(c, 1)
            pool.memset(identb[:, :], 0.0).then_inc(c, 1)
            pool.memset(sel[:, :, :], 0.0).then_inc(c, 1)
            pool.memset(ind[:, :], 1.0).then_inc(c, 1)
            pool.memset(mhalf[:, :], -0.5).then_inc(c, 1)
            pool.iota(iota8[:, :], pattern=[[1, E]], base=0, channel_multiplier=0,
                      allow_small_or_imprecise_dtypes=True).then_inc(c, 1)
            pool.memset(utri[:, :], 1.0).then_inc(c, 1)
            pool.memset(tri8[:, :, :], 1.0).then_inc(c, 1)
            pool.memset(onesb[:, :], 1.0).then_inc(c, 1)
            pool.iota(j128[:, :], pattern=[[P, NS]], base=0, channel_multiplier=0,
                      allow_small_or_imprecise_dtypes=True).then_inc(c, 1)
            pool.iota(jblk[:, :], pattern=[[1, NB]], base=0, channel_multiplier=0,
                      allow_small_or_imprecise_dtypes=True).then_inc(c, 1)
            pool.wait_ge(c, 11)
            for m in (identf, identb):
                pool.affine_select(out=m[:, :], in_=m[:, :], compare_op=ALU.not_equal, fill=1.0,
                                   base=0, pattern=[[-1, P]], channel_multiplier=1).then_inc(c, 1)
            pool.affine_select(out=sel[:, :, :], in_=sel[:, :, :], compare_op=ALU.not_equal, fill=1.0,
                               base=0, pattern=[[0, HC], [-1, S]], channel_multiplier=1).then_inc(c, 1)
            pool.affine_select(out=ind[:, :], in_=ind[:, :], compare_op=ALU.is_ge, fill=0.0,
                               base=0, pattern=[[-DK, HC]], channel_multiplier=1).then_inc(c, 1)
            pool.wait_ge(c, 15)
            pool.affine_select(out=sel[:, :, :], in_=sel[:, :, :], compare_op=ALU.not_equal, fill=1.0,
                               base=-S, pattern=[[-1, HC], [0, S]], channel_multiplier=1).then_inc(c, 1)
            pool.affine_select(out=ind[:, :], in_=ind[:, :], compare_op=ALU.is_ge, fill=0.0,
                               base=DK - 1, pattern=[[DK, HC]], channel_multiplier=-1).then_inc(c, 1)
            pool.affine_select(out=utri[:, :], in_=utri[:, :], compare_op=ALU.is_gt, fill=0.0,
                               base=0, pattern=[[1, P]], channel_multiplier=-1).then_inc(c, 1)
            pool.affine_select(out=tri8[:, :, :], in_=tri8[:, :, :], compare_op=ALU.is_gt, fill=0.0,
                               base=0, pattern=[[1, E], [-1, E]], channel_multiplier=0).then_inc(c, 1)

            def rsqrt1(b):
                pool.wait_ge(s("v_ve1"), b + 1)
                if b >= 1:
                    pool.wait_ge(s("v_xn"), b)
                pool.tensor_tensor(rs1[:, :], ve1[:, :], mhalf[:, :], ALU.pow).then_inc(s("g_r1"), 1)

            def add_bo(b):
                pool.wait_ge(s("v_xn"), b + 1)
                pool.tensor_tensor(xr[:, b, :, :], xr[:, b, :, :], bo_b[:, :].unsqueeze(1).to_broadcast([P, TH, D]),
                                   ALU.add).then_inc(s("g_xbo"), 1)

            def rsqrt2(b):
                pool.wait_ge(s("v_ve2"), b + 1)
                if b >= 1:
                    pool.wait_ge(s("v_hn"), b)
                pool.tensor_tensor(rs2[:, :], ve2[:, :], mhalf[:, :], ALU.pow).then_inc(s("g_r2"), 1)

            def scatter():
                pool.wait_ge(s("v_idx"), 1)
                pool.wait_ge(s("d_z"), 16)
                for t in range(NS):
                    pool.indirect_dma_start(scr_h, bass.IndirectOffsetOnAxis(ap=slot[:, t:t + 1], axis=0),
                                            hn[:, t, :], None).then_inc(s("d_sc"), 16)

            def gather():
                for i in range(HR):
                    pool.wait_ge(s(f"d_ys{i}"), 16 * len([j for j in range(NB) if j % HR == i]))
                for t in range(NS):
                    pool.indirect_dma_start(gy[:, t, :], None, scr_y,
                                            bass.IndirectOffsetOnAxis(ap=slot[:, t:t + 1], axis=0)).then_inc(s(f"d_gy{t}"), 16)

            def split_experts(n):
                k, e0 = n // EP, 2 * (n % EP)
                pool.wait_ge(s("d_e"), 16 * (k + 1))
                pool.tensor_copy(eH[:, k, e0:e0 + 2, :], e_nat[:, e0:e0 + 2, :]).then_inc(s("g_eH"), 1)
                pool.wait_ge(s("g_eH"), n + 1)
                pool.tensor_tensor(eL[:, k, e0:e0 + 2, :], e_nat[:, e0:e0 + 2, :],
                                   eH[:, k, e0:e0 + 2, :].bitcast(F32), ALU.subtract).then_inc(s("g_e"), 1)

            rsqrt1(0)
            pool.wait_ge(s("d_bias"), 16 * 8)
            add_bo(0)
            for i in ITER:
                if 0 < i + 2 < B:
                    rsqrt1(i + 2)
                    add_bo(i + 2)
                for n in {-2: [0, 1], -1: [2, 3], 1: [4], 2: [5], 3: [6], 4: [7]}.get(i, []):
                    split_experts(n)
                if 0 <= i - 1 < B:
                    rsqrt2(i - 1)
                if i - 2 == SB - 1:
                    scatter()
            gather()

        DENSE = {B: [[], [0], [1], [2], [], [3], [4], [5]],
                 B + 1: [[6], [], [7], [8], [9], [10], [11], [12, 13]]}
        SUMS = {B: [[], [], [], [], [], [0, 1, 2, 3], [4], [5]],
                B + 1: [[6], [], [7], [], [], [8, 9, 10], [11], [12, 13]]}
        STEPS = {B: [[], [], [], [], [], [0, 1], [2, 3, 4], [5, 6, 7, 8]],
                 B + 1: [[9, 10, 11, 12, 13], [14, 15, 16, 17], [18, 19, 20], [], [], [], [], []]}

        LOADS = {B: [[], [0, 1], [2, 3], [4, 5], [6, 7, 8], [9, 10, 11], [12, 13], [14, 15]],
                 B + 1: [[16, 17, 18], [], [], [], [], [], [], []]}

        def at(table, i, f):
            return table[i][f] if i in table else []

        def left(table, n):
            return range(max(sum(table[B + 1], [])) + 1, n)

        RTb = RT[:, 0:KC * T // 2].bitcast(BF16).rearrange("p (c t) -> p c t", c=KC)

        @block.tensor
        def _(pe):
            pe.wait_ge(s("c_pool"), 12)

            def three(out_ap, l, r):
                n = 0
                for k in range(KC):
                    for a, c in ((l[0], r[0]), (l[0], r[1]), (l[1], r[0])):
                        n += 1
                        t = pe.matmul(out_ap, a(k), c(k), start=(n == 1), stop=(n == 3 * KC))
                return t

            def turn4(src):
                for k in range(KC):
                    for h in range(TH):
                        t = pe.transpose(TRk[:, k, h * P:(h + 1) * P], src(h, k), identf[:, :])
                return t

            def a_ctx_turn(b):
                pe.wait_ge(s(f"d_c{b % 2}"), 16 * (b // 2 + 1))
                for k in range(KC):
                    t = pe.transpose(TR[:, k * S:(k + 1) * S], ctxs[:, b % 2, k * P:(k + 1) * P], identf[0:S, 0:S])
                t.then_inc(s("p_cT"), 1)

            def a_keys(b):
                pe.wait_ge(s("v_cL"), b + 1)
                for m in range(KC):
                    t = three(PJ[:, m * S:(m + 1) * S],
                              (lambda k: wH[:, 1, k, m * P:(m + 1) * P], lambda k: wL[:, 1, k, m * P:(m + 1) * P]),
                              (lambda k: cH[:, k, :], lambda k: cL[:, k, :]))
                t.then_inc(s("p_k"), 1)

            def a_values(b):
                if b == 0:
                    pe.wait_ge(s("v_w"), 2)
                t = three(TR[0:S, 0:D], (lambda k: cH[:, k, :], lambda k: cL[:, k, :]),
                          (lambda k: wH[:, 2, k, :], lambda k: wL[:, 2, k, :]))
                t.then_inc(s("p_v"), 1)

            def a_x_turn(b):
                pe.wait_ge(s("v_xn"), b + 1)
                turn4(lambda h, k: xn[:, h, k * P:(k + 1) * P]).then_inc(s("p_xT"), 1)

            def a_queries(b):
                pe.wait_ge(s("v_xL"), b + 1)
                if b == 0:
                    pe.wait_ge(s("v_w"), 4)
                for m in range(KC):
                    t = three(PJk[:, m, :],
                              (lambda k: wH[:, 0, k, m * P:(m + 1) * P], lambda k: wL[:, 0, k, m * P:(m + 1) * P]),
                              (lambda k: xH[:, k, :], lambda k: xL[:, k, :]))
                t.then_inc(s("p_q"), 1)

            def mx(b, i):
                h, c, q = i // 4, (i // 2) % 2, i % 2
                if i == 0:
                    pe.wait_ge(s("a_kb"), b + 1)
                    pe.wait_ge(s("v_tb"), b + 1)
                    pe.wait_ge(s("a_qH"), KC * (b + 1))
                n = NM * b + i
                if n >= 2:
                    pe.wait_ge(s("v_mx"), n - 1)
                o = MX[i % 2][:, 0:G * S]
                hd = c * HC + q * G
                pe.matmul(o, qH[:, b % 3, c, h * P:(h + 1) * P], kbH[:, b % 3, hd:hd + G, :], start=True, stop=False)
                pe.matmul(o, identb[:, :], tb[:, b % 2, h, 0, 0:S].unsqueeze(1).to_broadcast([P, G, S]),
                          start=False, stop=True).then_inc(s("p_mx"), 1)

            def turn_bias(b):
                pe.wait_ge(s("v_mx"), NM * (b + 1))
                pe.wait_ge(s("a_tb"), b + 1)
                for c in range(KC):
                    for h in range(TH):
                        t = pe.transpose(RTb[:, c, h * P:(h + 1) * P], tb[:, b % 2, h, c, :], identb[:, :])
                t.then_inc(s("p_T"), 1)

            def st(b, f):
                n = NF * b + f
                if f == 0:
                    pe.wait_ge(s("a_T"), b + 1)
                    pe.wait_ge(s("v_kbL"), b + 1)
                    pe.wait_ge(s("v_qL"), b + 1)
                if n >= 2:
                    pe.wait_ge(s("a_exp"), n - 1)
                for j in range(2):
                    hd = 2 * f + j
                    c = hd // HC
                    o = ST[f % 2][0:S, j * T:(j + 1) * T]
                    pe.matmul(o, kbH[:, b % 3, hd, :], qH[:, b % 3, c, :], start=True, stop=False)
                    pe.matmul(o, kbL[:, b % 2, hd, :], qH[:, b % 3, c, :], start=False, stop=False)
                    pe.matmul(o, kbH[:, b % 3, hd, :], qL[:, b % 3, c, :], start=False, stop=False)
                    t = pe.matmul(o, sel[:, hd % HC, :], tT[:, b % 2, c, :], start=False, stop=True)
                t.then_inc(s("p_st"), 1)

            def pv(b, g):
                pe.wait_ge(s("a_exp"), NF * b + 2 * g + 2)
                pe.wait_ge(s("v_va"), b + 1)
                if g % 2 == 0 and (b or g):
                    pe.wait_ge(s("a_ov"), 2 * b + g // 2)
                for j in range(G):
                    hd = G * g + j
                    t = pe.matmul(OVg[32 * j:32 * j + 32, g % 2, :], va[:, b % 3, hd, :, :],
                                  pr[:, (hd // 2) % PR, hd % 2, :], start=True, stop=True)
                t.then_inc(s("p_pv"), 1)

            def c_out_turn(b):
                pe.wait_ge(s("a_ov"), 2 * b + 2)
                for h, bank in enumerate((TR, PJ)):
                    if h == 0:
                        read("v_va", b + 3)
                        read("v_hL", b - 1)
                    else:
                        read("v_kL", b + 3)
                    for g in range(H // G):
                        t = pe.transpose(bank[:, g * P:(g + 1) * P], ou[:, g, h * P:(h + 1) * P], identf[:, :])
                    t.then_inc(s("p_ot"), 1)

            def c_norm_turn(b):
                pe.wait_ge(s("v_on"), TH * (b + 1))
                turn4(lambda h, k: on[:, h, k * P:(k + 1) * P]).then_inc(s("p_on"), 1)

            def c_project(b):
                pe.wait_ge(s("v_onL"), b + 1)
                for h in range(TH):
                    t = three(PJk[:, h, :],
                              (lambda k: oH[:, k, h * P:(h + 1) * P], lambda k: oL[:, k, h * P:(h + 1) * P]),
                              (lambda k: wH[:, 3, k, :], lambda k: wL[:, 3, k, :]))
                t.then_inc(s("p_op"), 1)

            def c_hidden_turn(b):
                pe.wait_ge(s("v_hn"), b + 1)
                turn4(lambda h, k: hn[:, TH * b + h, k * P:(k + 1) * P]).then_inc(s("p_hT"), 1)

            def c_logits(b):
                pe.wait_ge(s("v_hL"), b + 1)
                hi, lo = hidden_buf(b)
                t = three(RT[0:E, 0:T], (lambda k: rH[:, k, :], lambda k: rL[:, k, :]),
                          (lambda k: hi[:, k, :], lambda k: lo[:, k, :]))
                t.then_inc(s("p_lg"), 1)

            def r_turn(b):
                pe.wait_ge(s("a_lg"), b + 1)
                for h in range(TH):
                    t = pe.transpose(RT[:, h * E:(h + 1) * E], lgT[:, h * P:(h + 1) * P], identf[0:E, 0:E])
                t.then_inc(s("p_lt"), 1)

            def r_gates_turn(b):
                pe.wait_ge(s("v_dsp"), b + 1)
                for h in range(TH):
                    t = pe.transpose(RT[0:E, h * P:(h + 1) * P], dsp[:, b % 2, h, :], identf[:, :])
                t.then_inc(s("p_dT"), 1)

            def r_bias(b):
                for h in range(TH):
                    t = pe.matmul(RTk[:, h, :], dT[:, h * P:(h + 1) * P], eb[:, :], start=True, stop=True)
                t.then_inc(s("p_bs"), 1)

            def r_ranks():
                n = NS * E
                pe.matmul(RT[:, 0:n], utri[:, :], oh[:, 0:NS, :], start=True, stop=False)
                pe.matmul(RT[:, 0:n], onesb[:, :], cum[:, 0:NS, :], start=False, stop=True)
                pe.matmul(RT[:, n:n + E], onesb[:, :], cum[:, NS, :], start=True, stop=True).then_inc(s("p_rk"), 1)

            experts = {}

            def load_experts(js):
                for j in js:
                    if j == 0:
                        pe.wait_ge(s("v_be"), 1)
                    if j < NB:
                        experts[j] = pe.value_load(be[0:1, j:j + 1], min_val=0, max_val=E - 1)

            def block_step(j):
                if j < NB:
                    pe.wait_ge(s(f"d_hb{j % HR}"), 16 * (j // HR + 1))
                    if j >= 2:
                        pe.wait_ge(s("v_bL"), j - 1)
                    for k in range(KC):
                        t = pe.transpose(TURN[j % 2][:, k * P:(k + 1) * P], hb[:, j % HR, k * P:(k + 1) * P], identf[:, :])
                    t.then_inc(s("p_bT"), 1)
                if j >= 2:
                    m = j - 2
                    e = experts.pop(m)
                    pe.wait_ge(s("v_bL"), m + 1)
                    if m == 0:
                        pe.wait_ge(s("v_dn"), 3)
                    if m >= 2:
                        pe.wait_ge(s("a_y"), m - 1)
                    three(PROD[m % 2].rearrange("p (o d) -> p o d", o=1),
                          (lambda k: bH[:, m % 3, k, :], lambda k: bL[:, m % 3, k, :]),
                          (lambda k: eH[:, k, bass.ds(e, 1), :], lambda k: eL[:, k, bass.ds(e, 1), :])).then_inc(s("p_by"), 1)

            def dense_unit(u):
                b, p, h, bank = unit(u)
                if u == 0:
                    pe.wait_ge(s("g_e"), KC * EP)
                if u % NU == 0:
                    pe.wait_ge(s("v_hL"), b + 1)
                if u == 0:
                    pe.wait_ge(s("a_exp"), NF * B)
                    pe.wait_ge(s("a_ov"), 2 * B)
                if bank is PJ:
                    pe.wait_ge(s("v_x1"), B)
                if bank is TR:
                    pe.wait_ge(s("v_hL"), B)
                before = [w for w in range(u) if UB[w] is bank]
                if before:
                    pe.wait_ge(s("v_dn"), before[-1] + 1)
                hi, lo = hidden_buf(b)
                three(bank[:, :].rearrange("p (e d) -> p e d", e=2),
                      (lambda k: hi[:, k, h * P:(h + 1) * P], lambda k: lo[:, k, h * P:(h + 1) * P]),
                      (lambda k: eH[:, k, 2 * p:2 * p + 2, :], lambda k: eL[:, k, 2 * p:2 * p + 2, :])).then_inc(s("p_dn"), 1)

            def read(name, b, per=1):
                if 0 <= b < B:
                    pe.wait_ge(s(name), per * (b + 1))

            for n, i in enumerate(ORDER):
                pe.wait_ge(s(f"d_w{i}"), 16)
                for kin in range(KC):
                    for ko in range(KC):
                        t = pe.transpose(WB[i][:, kin * D + ko * P:kin * D + (ko + 1) * P],
                                         w_nat[:, i, ko, kin * P:(kin + 1) * P], identf[:, :])
                t.then_inc(s("p_w"), 1)
                if n == 1:
                    a_ctx_turn(0)
            pe.wait_ge(s("c_pool"), 19)
            for i in ITER:
                A, M, C, R = i + 2, i + 1, i - 1, i - 2
                isA, isM, isS, isC, isR = (0 <= n < B for n in (A, M, i, C, R))
                for f in range(NF):
                    if isS and f:
                        st(i, f)
                    if f == 6 and i + 3 < B:
                        read("v_onL", C)
                        read("v_xL", A)
                        a_ctx_turn(i + 3)
                    if isM:
                        for n in (MAXIMA if i >= 0 else FIRST_MAXIMA)[f]:
                            mx(M, n)
                    if f == 3 and isA:
                        read("v_va", A)
                        if isC:
                            pe.wait_ge(s("v_on"), TH * C + 1)
                        a_x_turn(A)
                    if f == 0:
                        if isC:
                            pv(C, 3)
                        if isA:
                            read("v_x1", R)
                            read("v_qL", M)
                            if i == -2:
                                pe.wait_ge(s("v_w"), 1)
                            a_keys(A)
                        if isS:
                            st(i, f)
                    if f == 1:
                        if isA:
                            read("v_hL", R)
                            a_values(A)
                        if isR:
                            read("a_T", i)
                            read("v_acc", R - 1)
                            if R == 0:
                                pe.wait_ge(s("v_r"), 1)
                            c_logits(R)
                    if f == 2:
                        if isC:
                            c_out_turn(C)
                        if isR:
                            r_turn(R)
                    if f == 3 and isS:
                        pv(i, 0)
                    if f == 4:
                        if isC:
                            read("v_xL", A)
                            c_norm_turn(C)
                        if isA:
                            read("v_kL", A)
                            a_queries(A)
                    if f == 5:
                        if isS:
                            pv(i, 1)
                        if isC:
                            read("v_qL", A)
                            c_project(C)
                        if R == SB - 1:
                            pe.wait_ge(s("v_dsp"), R + 1)
                            r_ranks()
                            pe.wait_ge(s("v_rk"), 1)
                        if isR:
                            r_gates_turn(R)
                    if f == 6:
                        if isR:
                            pe.wait_ge(s("a_dT"), R + 1)
                            r_bias(R)
                    if f == 7:
                        if isM:
                            read("v_acc", R)
                            turn_bias(M)
                        if isS:
                            pv(i, 2)
                        if isC:
                            read("v_cL", i + 3)
                            c_hidden_turn(C)
                    for u in at(DENSE, i, f):
                        dense_unit(u)
                    load_experts(at(LOADS, i, f))
                    for j in at(STEPS, i, f):
                        block_step(j)
            for j in left(STEPS, NB + 2):
                block_step(j)
            for u in left(DENSE, 2 * NU):
                dense_unit(u)

        @block.scalar
        def _(act):
            def block_part(j):
                if j < NB:
                    act.wait_ge(s("p_bT"), j + 1)
                    if j >= 3:
                        act.wait_ge(s("p_by"), j - 2)
                    act.activation(bH[:, j % 3, :, :], TURN[j % 2], ACT.Copy).then_inc(s("a_bH"), 1)
                if j >= 2:
                    m = j - 2
                    act.wait_ge(s("p_by"), m + 1)
                    if m == 0:
                        act.wait_ge(s("p_pv"), 4 * B)
                    if m >= HR:
                        act.wait_ge(s(f"d_ys{m % HR}"), 16 * (m // HR))
                    act.activation(yb[:, m % HR, :], PROD[m % 2], ACT.Copy).then_inc(s("a_y"), 1)

            def exp(b, f):
                n = NF * b + f
                act.wait_ge(s("p_st"), n + 1)
                if n >= PR:
                    act.wait_ge(s("p_pv"), (n - PR) // 2 + 1)
                act.activation(pr[:, f % PR, :, :], ST[f % 2][0:S, :], ACT.Exp, scale=SCALE).then_inc(s("a_exp"), 1)

            def out_copy(b, half):
                act.wait_ge(s("p_pv"), 4 * b + 2 * half + 2)
                if b >= 1:
                    act.wait_ge(s("p_ot"), TH * b)
                act.activation(ou[:, 2 * half:2 * half + 2, :], OVg, ACT.Copy).then_inc(s("a_ov"), 1)

            def ctx_high(b):
                act.wait_ge(s("p_cT"), b + 1)
                if b >= 1:
                    act.wait_ge(s("p_v"), b)
                act.activation(cH[:, :, :], TR[:, 0:KC * S], ACT.Copy).then_inc(s("a_cH"), 1)

            def keys_high(b):
                act.wait_ge(s("p_k"), b + 1)
                if b >= 1:
                    act.wait_ge(s("v_kL"), b)
                    act.wait_ge(s("a_kb"), b)
                for m in range(KC):
                    act.activation(kH[:, m, :], PJ[:, m * S:(m + 1) * S], ACT.Identity,
                                   bias=bk_c[:, m:m + 1]).then_inc(s("a_kH"), 1)

            def keys_masked(b, n0, n1):
                if n0 == 0:
                    act.wait_ge(s("a_kH"), KC * (b + 1))
                    if b >= 3:
                        act.wait_ge(s("p_st"), NF * (b - 2))
                for h in range(n0, n1):
                    a = act.activation(kbH[:, b % 3, h, :], kH[:, h // HC, :].bitcast(F32), ACT.Copy,
                                       scale=ind[:, h % HC:h % HC + 1])
                if n1 == H:
                    a.then_inc(s("a_kb"), 1)

            def x_high(b):
                act.wait_ge(s("p_xT"), b + 1)
                if b >= 1:
                    act.wait_ge(s("p_q"), b)
                act.activation(xH[:, :, :], TR[:, :], ACT.Copy).then_inc(s("a_xH"), 1)

            def queries_high(b):
                act.wait_ge(s("p_q"), b + 1)
                for m in range(KC):
                    act.activation(qH[:, b % 3, m, :], PJk[:, m, :], ACT.Identity,
                                   bias=bq_c[:, m:m + 1]).then_inc(s("a_qH"), 1)

            def gate_exp(b):
                act.wait_ge(s("v_lc"), b + 1)
                act.activation(le[:, :, :], lc[:, :, :], ACT.Exp).then_inc(s("a_le"), 1)

            def norm_high(b):
                act.wait_ge(s("p_on"), b + 1)
                if b >= 1:
                    act.wait_ge(s("p_op"), b)
                act.activation(oH[:, :, :], TR[:, :], ACT.Copy).then_inc(s("a_onH"), 1)

            def hidden_high(b):
                act.wait_ge(s("p_hT"), b + 1)
                if b >= 1:
                    act.wait_ge(s("p_lg"), b)
                act.activation(hidden_buf(b)[0][:, :, :], TR[:, :], ACT.Copy).then_inc(s("a_hH"), 1)

            def bias_copy(b):
                act.wait_ge(s("p_T"), b + 1)
                if b >= 2:
                    act.wait_ge(s("p_st"), NF * (b - 1))
                act.activation(tT[:, b % 2, :, :], RTb, ACT.Copy).then_inc(s("a_T"), 1)

            def bias_double(b):
                act.wait_ge(s("v_tb"), b + 1)
                act.activation(tb[:, b % 2, :, 1, 0:S], tb[:, b % 2, :, 0, 0:S], ACT.Copy).then_inc(s("a_tb"), 1)

            def gates_copy(b):
                act.wait_ge(s("p_dT"), b + 1)
                act.activation(dT[:, :], RT[0:E, 0:T], ACT.Copy).then_inc(s("a_dT"), 1)

            def logits_copy(b):
                act.wait_ge(s("p_lg"), b + 1)
                act.activation(lgT[:, :], RT[0:E, 0:T], ACT.Copy).then_inc(s("a_lg"), 1)

            for n, i in enumerate(ORDER):
                act.wait_ge(s("p_w"), n + 1)
                act.activation(wH[:, i, :, :], WB[i][:, :], ACT.Copy).then_inc(s("a_w"), 1)
                if n == 1:
                    ctx_high(0)
            act.wait_ge(s("d_bias"), 16 * 8)
            act.wait_ge(s("c_pool"), 19)
            EARLY = [0, 0, 6, 10, 13, H, H, H, H]
            MASKED = [0, 0, 3, 6, 9, 12, 15, H, H]
            for i in ITER:
                A, M, C, R = i + 2, i + 1, i - 1, i - 2
                isA, isM, isS, isC, isR = (0 <= n < B for n in (A, M, i, C, R))
                for f in range(NF):
                    if f == 0:
                        if isC:
                            out_copy(C, 1)
                        if isA:
                            keys_high(A)
                    if isS:
                        exp(i, f)
                    if f == 1 and isR:
                        logits_copy(R)
                    if f == 2 and isM:
                        bias_double(M)
                    if f == 3 and isA:
                        x_high(A)
                    if f == 4:
                        if isR:
                            gate_exp(R)
                        if isC:
                            norm_high(C)
                        if isA:
                            queries_high(A)
                    if f == 5:
                        if isS:
                            out_copy(i, 0)
                        if isR:
                            gates_copy(R)
                    if f == 6 and i + 3 < B:
                        ctx_high(i + 3)
                    if f == 7:
                        if isM:
                            bias_copy(M)
                        if isC:
                            hidden_high(C)
                    masked = EARLY if i < 0 else MASKED
                    if isA and masked[f + 1] > masked[f]:
                        keys_masked(A, masked[f], masked[f + 1])
                    for j in at(STEPS, i, f):
                        block_part(j)
                if i == -1:
                    act.activation(rH[:, :, :], r_nat[:, :, :], ACT.Copy).then_inc(s("a_r"), 1)
            for j in left(STEPS, NB + 2):
                block_part(j)

        @block.vector
        def _(v):
            cnt = [0]

            def link(ins):
                cnt[0] += 1
                ins.then_inc(s("dve"), 1)
                v.wait_ge(s("dve"), cnt[0])

            v.memset(zer[:, :], 0.0).then_inc(s("c_dve"), 1)
            v.memset(va[:, :, :, 1, :], 1.0).then_inc(s("c_dve"), 1)
            v.memset(cum[:, :, :], 0.0).then_inc(s("c_dve"), 1)
            v.wait_ge(s("c_pool"), 19)

            def ln_stats(src, stt, mvt, vet, name):
                for h in range(TH):
                    i = v.bn_stats(stt[:, h, :], src(h))
                link(i)
                for h in range(TH):
                    i = v.bn_aggr(mvt[:, h, :], stt[:, h, :])
                link(i)
                v.tensor_scalar(vet[:, :], mvt[:, :, 1], EPS, None, ALU.add).then_inc(s(name), 1)

            def ln1_stats(b):
                v.wait_ge(s(f"d_x{b}"), 16)
                if b >= 1:
                    v.wait_ge(s("g_r1"), b)
                ln_stats(lambda h: xr[:, b, h, :], st1, mv1, ve1, "v_ve1")

            def ln1_apply(b):
                v.wait_ge(s("g_r1"), b + 1)
                if b >= 1:
                    v.wait_ge(s("p_xT"), b)
                for h in range(TH):
                    i = v.tensor_scalar(xn[:, h, :], xr[:, b, h, :], mv1[:, h, 0:1], rs1[:, h:h + 1],
                                        ALU.subtract, ALU.mult)
                i.then_inc(s("v_xn"), 1)

            def ctx_low(bn):
                v.wait_ge(s("a_cH"), bn + 1)
                v.tensor_tensor(cL[:, :, :], TR[:, 0:KC * S].rearrange("p (k s) -> p k s", k=KC),
                                cH[:, :, :].bitcast(F32), ALU.subtract).then_inc(s("v_cL"), 1)

            def keys_values(bn):
                pn = bn % 3
                v.wait_ge(s("a_kH"), KC * (bn + 1))
                for m in range(KC):
                    i = v.scalar_tensor_tensor(out=kL[:, bn % 2, m, :], in0=PJ[:, m * S:(m + 1) * S],
                                               scalar=bk_c[:, m:m + 1], in1=kH[:, m, :].bitcast(F32),
                                               op0=ALU.add, op1=ALU.subtract)
                i.then_inc(s("v_kL"), 1)
                v.wait_ge(s("p_v"), bn + 1)
                if bn >= 3:
                    v.wait_ge(s("p_pv"), 4 * (bn - 2))
                v.tensor_tensor(va[:, pn, :, 0, :], TR[0:S, 0:D].rearrange("p (h d) -> p h d", h=H),
                                bv_b[0:S, :].rearrange("p (h d) -> p h d", h=H), ALU.add).then_inc(s("v_va"), 1)

            def keys_low(bn):
                v.wait_ge(s("v_kL"), bn + 1)
                if bn >= 2:
                    v.wait_ge(s("p_st"), NF * (bn - 1))
                for m in range(KC):
                    i = v.tensor_tensor(kbL[:, bn % 2, m * HC:(m + 1) * HC, :],
                                        kL[:, bn % 2, m, :].unsqueeze(1).to_broadcast([P, HC, S]),
                                        ind[:, :].unsqueeze(2).to_broadcast([P, HC, S]), ALU.mult)
                i.then_inc(s("v_kbL"), 1)

            def mask_bias(bn):
                pn = bn % 2
                v.wait_ge(s(f"d_k{pn}"), 16 * (bn // 2 + 1))
                if bn >= 2:
                    v.wait_ge(s("p_T"), bn - 1)
                v.scalar_tensor_tensor(out=tb[:, pn, :, 0, 0:S],
                                       in0=kp8[:, pn, :].unsqueeze(1).to_broadcast([P, TH, S]),
                                       scalar=-BIG, in1=attnb[:, :, :], op0=ALU.mult, op1=ALU.add).then_inc(s("v_tb"), 1)

            def empty_rows(b):
                v.wait_ge(s("v_mx"), NM * (b + 1))
                link(v.tensor_scalar(mg[:, :], tb[:, b % 2, :, 0, S], BIG / 2, None, ALU.is_lt))
                link(v.reciprocal(mr[:, :], mg[:, :]))
                link(v.tensor_tensor(nanf[:, b % 2, :], mg[:, :], mr[:, :], ALU.mult))

            def x_low(bn):
                v.wait_ge(s("a_xH"), bn + 1)
                v.tensor_tensor(xL[:, :, :], TRk, xH[:, :, :].bitcast(F32), ALU.subtract).then_inc(s("v_xL"), 1)

            def queries_low(bn):
                pn = bn % 3
                v.wait_ge(s("a_qH"), KC * (bn + 1))
                if bn >= 3:
                    v.wait_ge(s("p_st"), NF * (bn - 2))
                for m in range(KC):
                    i = v.scalar_tensor_tensor(out=qL[:, pn, m, :], in0=PJk[:, m, :], scalar=bq_c[:, m:m + 1],
                                               in1=qH[:, pn, m, :].bitcast(F32), op0=ALU.add, op1=ALU.subtract)
                i.then_inc(s("v_qL"), 1)

            def route_logits(b):
                v.wait_ge(s("p_lt"), b + 1)
                link(v.tensor_tensor(lg[:, :, :], RT[:, 0:TH * E].rearrange("p (h e) -> p h e", h=TH),
                                     rb_b[:, :].unsqueeze(1).to_broadcast([P, TH, E]), ALU.add))
                for h in range(TH):
                    i = v.max(mx8[:, h, :], lg[:, h, :])
                link(i)
                v.tensor_tensor(lc[:, :, :], lg[:, :, :], mx8[:, :, 0:1].to_broadcast([P, TH, E]),
                                ALU.subtract).then_inc(s("v_lc"), 1)
                for h in range(TH):
                    i = v.max_index(ix8[:, h, :], mx8[:, h, :], lg[:, h, :])
                link(i)
                link(v.tensor_copy(ixf[:, :], ix8[:, :, 0]))

            def route_choice(b):
                for h in range(TH):
                    i = v.tensor_scalar(oh[:, TH * b + h, :], iota8[:, :], ixf[:, h:h + 1], None, ALU.is_equal)
                link(i)
                if b < SB:
                    for h in range(TH):
                        t = TH * b + h
                        link(v.tensor_tensor(cum[:, t + 1, :], cum[:, t, :], oh[:, t, :], ALU.add))
                v.wait_ge(s("a_le"), b + 1)
                link(v.tensor_reduce(sm[:, :], le[:, :, :], AX_X, ALU.add))
                link(v.reciprocal(gts[:, TH * b:TH * b + TH], sm[:, :]))
                for h in range(TH):
                    i = v.tensor_scalar(dsp[:, b % 2, h, :], oh[:, TH * b + h, :], gts[:, TH * b + h:TH * b + h + 1], None, ALU.mult)
                i.then_inc(s("v_dsp"), 1)

            def add_bias(b):
                v.wait_ge(s("p_bs"), b + 1)
                v.tensor_tensor(xr[:, b, :, :], xr[:, b, :, :], RTk, ALU.add).then_inc(s("v_acc"), 1)

            def ranks_copy():
                v.wait_ge(s("p_rk"), 1)
                v.tensor_copy(tot[:, :], RT[:, NS * E:NS * E + E])
                v.tensor_copy(rk[:, :, :], RT[:, 0:NS * E].rearrange("p (t e) -> p t e", t=NS)).then_inc(s("v_rk"), 1)

            def places():
                v.wait_ge(s("v_rk"), 1)
                link(v.tensor_tensor(cmpn[:, :, :], tot[:, :].unsqueeze(2).to_broadcast([P, E, NS]),
                                     j128[:, :].unsqueeze(1).to_broadcast([P, E, NS]), ALU.is_gt))
                link(v.tensor_reduce(nblk[:, :], cmpn[:, :, :], AX_X, ALU.add))
                link(v.tensor_tensor(trin[:, :, :], tri8[:, :, :], nblk[:, :].unsqueeze(1).to_broadcast([P, E, E]), ALU.mult))
                link(v.tensor_reduce(sbk[:, :], trin[:, :, :], AX_X, ALU.add))
                v.tensor_scalar(base[:, :], sbk[:, :], float(P), None, ALU.mult)
                link(v.tensor_tensor(endb[:, :], sbk[:, :], nblk[:, :], ALU.add))
                link(v.tensor_tensor(rk2[:, :, :], rk[:, :, :], base[:, :].unsqueeze(1).to_broadcast([P, NS, E]), ALU.add))
                link(v.tensor_tensor(rk[:, :, :], rk2[:, :, :], oh[:, 0:NS, :], ALU.mult))
                link(v.tensor_reduce(slotf[:, :], rk[:, :, :], AX_X, ALU.add))
                v.tensor_copy(slot[:, :], slotf[:, :]).then_inc(s("v_idx"), 1)
                link(v.tensor_tensor(cmpb[:, :, :], endb[:, :].unsqueeze(1).to_broadcast([P, NB, E]),
                                     jblk[:, :].unsqueeze(2).to_broadcast([P, NB, E]), ALU.is_le))
                link(v.tensor_reduce(bef[:, :], cmpb[:, :, :], AX_X, ALU.add))
                v.tensor_scalar(be[:, :], bef[:, :], float(E - 1), None, ALU.min).then_inc(s("v_be"), 1)

            def maxima(b, i):
                h, c, q = i // 4, (i // 2) % 2, i % 2
                v.wait_ge(s("p_mx"), NM * b + i + 1)
                v.tensor_reduce(tb[:, b % 2, h, c, S + q * G:S + (q + 1) * G],
                                MX[i % 2][:, 0:G * S].rearrange("p (g s) -> p g s", g=G),
                                AX_X, ALU.max, negate=True).then_inc(s("v_mx"), 1)

            def normalise(b):
                if b >= 1:
                    v.wait_ge(s("p_on"), b)
                o4 = [bank[:, :].rearrange("p (n z d) -> p n z d", n=H, z=2) for bank in (TR, PJ)]
                for h in range(TH):
                    v.wait_ge(s("p_ot"), TH * b + h + 1)
                    i = v.reciprocal(rd[:, h, :], o4[h][:, :, 1, 0])
                link(i)
                for h in range(TH):
                    i = v.tensor_scalar(rdn[:, h, :], rd[:, h, :], nanf[:, b % 2, h:h + 1], None, ALU.mult)
                link(i)
                for h in range(TH):
                    v.tensor_tensor(on[:, h, :].rearrange("p (n d) -> p n d", n=H), o4[h][:, :, 0, :],
                                    rdn[:, h, :].unsqueeze(2).to_broadcast([P, H, DK]),
                                    ALU.mult).then_inc(s("v_on"), 1)

            def norm_low(b):
                v.wait_ge(s("a_onH"), b + 1)
                v.tensor_tensor(oL[:, :, :], TRk, oH[:, :, :].bitcast(F32), ALU.subtract).then_inc(s("v_onL"), 1)

            def residual(b):
                v.wait_ge(s("p_op"), b + 1)
                v.wait_ge(s("g_xbo"), b + 1)
                v.tensor_tensor(xr[:, b, :, :], xr[:, b, :, :], PJk, ALU.add).then_inc(s("v_x1"), 1)
                v.wait_ge(s("v_x1"), b + 1)
                if b >= 1:
                    v.wait_ge(s("g_r2"), b)
                ln_stats(lambda h: xr[:, b, h, :], st2, mv2, ve2, "v_ve2")

            def hidden(b):
                v.wait_ge(s("g_r2"), b + 1)
                for h in range(TH):
                    ins = v.tensor_scalar(hn[:, TH * b + h, :], xr[:, b, h, :], mv2[:, h, 0:1], rs2[:, h:h + 1],
                                          ALU.subtract, ALU.mult)
                ins.then_inc(s("v_hn"), 1)

            def hidden_low(b):
                v.wait_ge(s("a_hH"), b + 1)
                hi, lo = hidden_buf(b)
                v.tensor_tensor(lo[:, :, :], TRk, hi[:, :, :].bitcast(F32), ALU.subtract).then_inc(s("v_hL"), 1)

            def block_part(j):
                if j < NB:
                    v.wait_ge(s("a_bH"), j + 1)
                    v.tensor_tensor(bL[:, j % 3, :, :], TURN[j % 2].rearrange("p (k t) -> p k t", k=KC),
                                    bH[:, j % 3, :, :].bitcast(F32), ALU.subtract).then_inc(s("v_bL"), 1)

            def dense_part(u):
                b, p, h, bank = unit(u)
                v.wait_ge(s("v_dsp"), b + 1)
                v.wait_ge(s("p_dn"), u + 1)
                for e in range(2):
                    i = v.scalar_tensor_tensor(out=xr[:, b, h, :], in0=bank[:, e * D:(e + 1) * D],
                                               scalar=dsp[:, b % 2, h, 2 * p + e:2 * p + e + 1],
                                               in1=xr[:, b, h, :], op0=ALU.mult, op1=ALU.add)
                    if e == 0:
                        link(i)
                i.then_inc(s("v_dn"), 1)
                v.wait_ge(s("v_dn"), u + 1)

            def finish(t):
                v.wait_ge(s(f"d_gy{t}"), 16)
                b, h = t // TH, t % TH
                v.scalar_tensor_tensor(out=xr[:, b, h, :], in0=gy[:, t, :], scalar=gts[:, t:t + 1],
                                       in1=xr[:, b, h, :], op0=ALU.mult, op1=ALU.add).then_inc(s("v_fin"), 1)

            ln1_stats(0)
            for n, i in enumerate(ORDER):
                v.wait_ge(s("a_w"), n + 1)
                v.tensor_tensor(wL[:, i, :, :], WB[i][:, :].rearrange("p (k d) -> p k d", k=KC),
                                wH[:, i, :, :].bitcast(F32), ALU.subtract).then_inc(s("v_w"), 1)
                if n == 1:
                    v.wait_ge(s("a_cH"), 1)
                    ctx_low(0)
                if n == 2:
                    ln1_apply(0)
            v.wait_ge(s("d_bias"), 16 * 8)
            link(v.tensor_scalar(attnb[:, :, :], am8[:, :, :], -BIG, None, ALU.mult))
            for i in ITER:
                A, M, C, R = i + 2, i + 1, i - 1, i - 2
                isA, isM, isS, isC, isR = (0 <= n < B for n in (A, M, i, C, R))
                for f in range(NF):
                    if f == 0 and isR:
                        hidden_low(R)
                    if f == 5:
                        if isA:
                            queries_low(A)
                        if isR:
                            route_choice(R)
                    if f == 6 and isC:
                        residual(C)
                    if f == 6 and R == SB - 1:
                        places()
                    if isM:
                        for n in (MAXIMA if i >= 0 else FIRST_MAXIMA)[f]:
                            maxima(M, n)
                    if f == 0 and isM:
                        keys_low(M)
                    if f == 1 and isA:
                        keys_values(A)
                        if A:
                            ln1_stats(A)
                    if f == 2:
                        if A and isA:
                            ln1_apply(A)
                        if isC:
                            normalise(C)
                    if f == 3:
                        if isA:
                            x_low(A)
                        if isR:
                            route_logits(R)
                    if f == 4:
                        if isC:
                            norm_low(C)
                    if f == (5 if i >= 0 else 1) and isA:
                        mask_bias(A)
                    if f == 5 and R == SB - 1:
                        ranks_copy()
                    if f == 7:
                        if isR:
                            add_bias(R)
                            v.wait_ge(s("v_acc"), R + 1)
                        if i + 3 < B:
                            ctx_low(i + 3)
                        if isC:
                            hidden(C)
                        if isM:
                            empty_rows(M)
                    for u in at(SUMS, i, f):
                        dense_part(u)
                    for j in at(STEPS, i, f):
                        block_part(j)
                if i == -1:
                    v.wait_ge(s("a_r"), 1)
                    v.tensor_tensor(rL[:, :, :], r_nat[:, :, :], rH[:, :, :].bitcast(F32), ALU.subtract).then_inc(s("v_r"), 1)
            for j in left(STEPS, NB + 2):
                block_part(j)
            for u in left(SUMS, 2 * NU):
                dense_part(u)
            for t in range(NS):
                finish(t)


_INS = ['x', 'ctx_1024', 'mask_SxS2_bk1', 'mask_BxS2_bf0', 'L0_xattn_Wq', 'L0_xattn_bq', 'L0_xattn_Wk',
        'L0_xattn_bk', 'L0_xattn_Wv', 'L0_xattn_bv', 'L0_xattn_Wo', 'L0_xattn_bo', 'L0_ffn_router_w',
        'L0_ffn_router_b', 'L0_ffn_expert_w', 'L0_ffn_expert_b']
_OUTS = [((8, 256, 256), 'float32')]


def kernel(**inputs):
    import numpy as _np
    import concourse.bacc as _bacc
    from concourse import mybir as _mybir
    from concourse.bass_utils import run_bass_kernel_spmd as _run

    nc = _bacc.Bacc("TRN2", target_bir_lowering=False, num_devices=1)
    arrays, args = {}, []
    for name in _INS:
        a = _np.ascontiguousarray(inputs[name])
        arrays[f"in_{name}_dram"] = a
        args.append(nc.dram_tensor(f"in_{name}_dram", a.shape, _mybir.dt.from_np(a.dtype), kind="ExternalInput").ap())
    for i, (shape, dtype) in enumerate(_OUTS):
        dt = _mybir.dt.from_np(_np.dtype(dtype))
        args.append(nc.dram_tensor(f"out_{i}_dram", shape, dt, kind="ExternalOutput").ap())
    xattn_moe_kernel(nc, *args)
    r = _run(nc, [arrays], core_ids=[0])
    return r.results[0]["out_0_dram"]
```
